# Optimizing a Trainium2 kernel written in Bass

```python
import numpy as np
import jax
import jax.numpy as jnp

def _softmax(x, axis=-1):
    return jax.nn.softmax(x, axis=axis)

def _gelu(x):
    return jax.nn.gelu(x, approximate=True)

def _silu(x):
    return jax.nn.silu(x)

def _sigmoid(x):
    return jax.nn.sigmoid(x)

def _layernorm(x, axis=-1, eps=1e-05):
    m = jnp.mean(x, axis=axis, keepdims=True)
    v = jnp.var(x, axis=axis, keepdims=True)
    return (x - m) / jnp.sqrt(v + eps)

def _scatter_add(tgt, idx, src, axis=0):
    return tgt.at[idx].add(src)

def _segment_sum(src, seg, n):
    return jax.ops.segment_sum(src, seg, n)
kernel_name = 'mk_adj_seq_d4_adj_r2_d8ed0b'

def setup_inputs(seed: int=0):
    np.random.seed(seed)
    _w = jnp.asarray

    def _rec_inputs():
        import jax
        import jax.numpy as jnp
        _gk = jax.random.key(seed)
        x = -0.0005207 + 1.001 * jax.random.normal(jax.random.fold_in(_gk, 1), (64, 128, 256), jnp.float32)
        _w = (1.0 + jnp.arange(128, dtype=jnp.float32)) ** (-0.5)
        _w = _w / _w.mean()
        _pij = jnp.clip(0.015625 * _w[:, None] * _w[None, :], 0.0, 1.0)
        _a = jax.random.uniform(jax.random.fold_in(_gk, 2), (64, 128, 128)) < _pij
        _a = jnp.logical_or(_a, jnp.eye(128, dtype=bool))
        adj = _a.astype(jnp.int32)
        return (x, adj)
    x, adj = _rec_inputs()

    def _L0_gnn_setup():
        import jax, jax.numpy as jnp
        import numpy as np
        B, S, D, H = (2, 1024, 256, 8)
        HD = D // H
        EPS = 1e-05

        def _ln(x, g, b):
            mu = jnp.mean(x, axis=-1, keepdims=True)
            var = jnp.mean((x - mu) ** 2, axis=-1, keepdims=True)
            return (x - mu) * jax.lax.rsqrt(var + EPS) * g + b
        key = jax.random.key(seed)
        ks = jax.random.split(key, 16)
        x = jax.random.normal(ks[0], (B, S, D), dtype=jnp.float32)
        adj = jax.random.randint(ks[1], (B, S, S), 0, 2, dtype=jnp.int32)
        adj = adj.at[:, jnp.arange(S), jnp.arange(S)].set(1)
        edge_attr = jax.random.normal(ks[2], (B, S, S), dtype=jnp.float32)
        sc = 1.0 / np.sqrt(D)
        p = lambda k, shp: jax.random.normal(k, shp, dtype=jnp.float32) * sc
        return {'x': x, 'adj_matrix': adj, 'edge_attr_matrix': edge_attr, 'ln1_g': jnp.ones((D,)), 'ln1_b': jnp.zeros((D,)), 'ln2_g': jnp.ones((D,)), 'ln2_b': jnp.zeros((D,)), 'wq': p(ks[3], (D, D)), 'bq': jnp.zeros((D,)), 'wk': p(ks[4], (D, D)), 'bk': jnp.zeros((D,)), 'wv': p(ks[5], (D, D)), 'bv': jnp.zeros((D,)), 'wo': p(ks[6], (D, D)), 'bo': jnp.zeros((D,)), 'w1': p(ks[7], (D, 4 * D)), 'b1': jnp.zeros((4 * D,)), 'w2': p(ks[8], (4 * D, D)), 'b2': jnp.zeros((D,))}
    _L0_gnn_all = _L0_gnn_setup()
    _L0_gnn_in = {k: v for k, v in _L0_gnn_all.items() if k in ('ln1_g', 'ln1_b', 'ln2_g', 'ln2_b', 'wq', 'bq', 'wk', 'bk', 'wv', 'bv', 'wo', 'bo', 'w1', 'b1', 'w2', 'b2')}
    del _L0_gnn_all

    def _L1_gnn_setup():
        import jax, jax.numpy as jnp
        import numpy as np
        B, N, E, FF, L = (8, 1024, 256, 128, 2)
        LN_EPS = 1e-05
        SCALE = float(np.sqrt(FF))

        def layer_norm(x, g, b):
            m = jnp.mean(x, axis=-1, keepdims=True)
            v = jnp.mean(jnp.square(x - m), axis=-1, keepdims=True)
            return (x - m) * jax.lax.rsqrt(v + LN_EPS) * g + b
        key = jax.random.key(seed)
        ks = jax.random.split(key, 9)
        s = 0.02
        node_fts = jax.random.normal(ks[0], (B, N, E), jnp.float32)
        rel_edges = jax.random.randint(ks[1], (B, N, N), 0, 2, jnp.int32)
        Wq = jax.random.normal(ks[2], (L, FF, E), jnp.float32) * s
        bq = jnp.zeros((L, FF), jnp.float32)
        Wk = jax.random.normal(ks[3], (L, FF, E), jnp.float32) * s
        bk = jnp.zeros((L, FF), jnp.float32)
        Wc = jax.random.normal(ks[4], (L, E, E), jnp.float32) * s
        ln_g = jnp.ones((L, E), jnp.float32)
        ln_b = jnp.zeros((L, E), jnp.float32)
        return {'node_fts': node_fts, 'rel_edges': rel_edges, 'Wq': Wq, 'bq': bq, 'Wk': Wk, 'bk': bk, 'Wc': Wc, 'ln_g': ln_g, 'ln_b': ln_b}
    _L1_gnn_all = _L1_gnn_setup()
    _L1_gnn_in = {k: v for k, v in _L1_gnn_all.items() if k in ('Wq', 'bq', 'Wk', 'bk', 'Wc', 'ln_g', 'ln_b')}
    del _L1_gnn_all

    def _L2_gnn_setup():
        import jax, jax.numpy as jnp
        import numpy as np
        import math
        D = 256
        B, L = (8, 1024)
        EPS = 1e-05

        def layer_norm(y, gamma, beta):
            mu = jnp.mean(y, axis=-1, keepdims=True)
            var = jnp.mean(jnp.square(y - mu), axis=-1, keepdims=True)
            return (y - mu) * jax.lax.rsqrt(var + EPS) * gamma + beta
        key = jax.random.key(seed)
        ks = jax.random.split(key, 8)
        s = 1.0 / math.sqrt(D)
        x = jax.random.normal(ks[0], (B, L, D), dtype=jnp.float32)
        adj = jax.random.randint(ks[1], (B, L, L), 0, 2, dtype=jnp.int32)
        Wq = jax.random.normal(ks[2], (D, D), dtype=jnp.float32) * s
        Wk = jax.random.normal(ks[3], (D, D), dtype=jnp.float32) * s
        Wv = jax.random.normal(ks[4], (D, D), dtype=jnp.float32) * s
        Wo = jax.random.normal(ks[5], (D, D), dtype=jnp.float32) * s
        bo = jnp.zeros((D,), dtype=jnp.float32)
        gamma = jnp.ones((D,), dtype=jnp.float32)
        beta = jnp.zeros((D,), dtype=jnp.float32)
        return {'x': x, 'adj': adj, 'Wq': Wq, 'Wk': Wk, 'Wv': Wv, 'Wo': Wo, 'bo': bo, 'gamma': gamma, 'beta': beta}
    _L2_gnn_all = _L2_gnn_setup()
    _L2_gnn_in = {k: v for k, v in _L2_gnn_all.items() if k in ('Wq', 'Wk', 'Wv', 'Wo', 'bo', 'gamma', 'beta')}
    del _L2_gnn_all

    def _L3_gnn_setup():
        import jax, jax.numpy as jnp
        import numpy as np
        B, N, H, D = (8, 512, 256, 4)
        EPS = 1e-08
        LN_EPS = 1e-05

        def _linear(x, W, b):
            return x @ W.T + b
        key = jax.random.key(seed)
        ks = jax.random.split(key, 20)
        inp = {'adj': jax.random.randint(ks[0], (B, N, N), 0, D + 1, dtype=jnp.int32), 'relative_pos': jax.random.randint(ks[1], (B, N, N), 0, 16, dtype=jnp.int32), 'hid': jax.random.normal(ks[2], (B, N, H), dtype=jnp.float32), 'Wd': jax.random.normal(ks[3], (H, D * H), dtype=jnp.float32) * (1.0 / np.sqrt(D * H)), 'bd': jnp.zeros((H,), jnp.float32)}
        s = 1.0 / np.sqrt(H)
        for i, nm in enumerate(['ri', 'rh', 'zi', 'zh', 'ni', 'nh']):
            inp['W' + nm] = jax.random.normal(ks[4 + i], (H, H), dtype=jnp.float32) * s
            inp['b' + nm] = jnp.zeros((H,), jnp.float32)
        inp['gamma'] = jnp.ones((H,), jnp.float32)
        inp['beta'] = jnp.zeros((H,), jnp.float32)
        return inp
    _L3_gnn_all = _L3_gnn_setup()
    _L3_gnn_in = {k: v for k, v in _L3_gnn_all.items() if k in ('Wd', 'bd', 'Wri', 'bri', 'Wrh', 'brh', 'Wzi', 'bzi', 'Wzh', 'bzh', 'Wni', 'bni', 'Wnh', 'bnh', 'gamma', 'beta')}
    del _L3_gnn_all
    return {'x': x, 'adj': adj, 'L0_gnn_ln1_g': _L0_gnn_in['ln1_g'], 'L0_gnn_ln1_b': _L0_gnn_in['ln1_b'], 'L0_gnn_ln2_g': _L0_gnn_in['ln2_g'], 'L0_gnn_ln2_b': _L0_gnn_in['ln2_b'], 'L0_gnn_wq': _L0_gnn_in['wq'], 'L0_gnn_bq': _L0_gnn_in['bq'], 'L0_gnn_wk': _L0_gnn_in['wk'], 'L0_gnn_bk': _L0_gnn_in['bk'], 'L0_gnn_wv': _L0_gnn_in['wv'], 'L0_gnn_bv': _L0_gnn_in['bv'], 'L0_gnn_wo': _L0_gnn_in['wo'], 'L0_gnn_bo': _L0_gnn_in['bo'], 'L0_gnn_w1': _L0_gnn_in['w1'], 'L0_gnn_b1': _L0_gnn_in['b1'], 'L0_gnn_w2': _L0_gnn_in['w2'], 'L0_gnn_b2': _L0_gnn_in['b2'], 'L1_gnn_Wq': _L1_gnn_in['Wq'], 'L1_gnn_bq': _L1_gnn_in['bq'], 'L1_gnn_Wk': _L1_gnn_in['Wk'], 'L1_gnn_bk': _L1_gnn_in['bk'], 'L1_gnn_Wc': _L1_gnn_in['Wc'], 'L1_gnn_ln_g': _L1_gnn_in['ln_g'], 'L1_gnn_ln_b': _L1_gnn_in['ln_b'], 'L2_gnn_Wq': _L2_gnn_in['Wq'], 'L2_gnn_Wk': _L2_gnn_in['Wk'], 'L2_gnn_Wv': _L2_gnn_in['Wv'], 'L2_gnn_Wo': _L2_gnn_in['Wo'], 'L2_gnn_bo': _L2_gnn_in['bo'], 'L2_gnn_gamma': _L2_gnn_in['gamma'], 'L2_gnn_beta': _L2_gnn_in['beta'], 'L3_gnn_Wd': _L3_gnn_in['Wd'], 'L3_gnn_bd': _L3_gnn_in['bd'], 'L3_gnn_Wri': _L3_gnn_in['Wri'], 'L3_gnn_bri': _L3_gnn_in['bri'], 'L3_gnn_Wrh': _L3_gnn_in['Wrh'], 'L3_gnn_brh': _L3_gnn_in['brh'], 'L3_gnn_Wzi': _L3_gnn_in['Wzi'], 'L3_gnn_bzi': _L3_gnn_in['bzi'], 'L3_gnn_Wzh': _L3_gnn_in['Wzh'], 'L3_gnn_bzh': _L3_gnn_in['bzh'], 'L3_gnn_Wni': _L3_gnn_in['Wni'], 'L3_gnn_bni': _L3_gnn_in['bni'], 'L3_gnn_Wnh': _L3_gnn_in['Wnh'], 'L3_gnn_bnh': _L3_gnn_in['bnh'], 'L3_gnn_gamma': _L3_gnn_in['gamma'], 'L3_gnn_beta': _L3_gnn_in['beta']}

def reference(x, adj, L0_gnn_ln1_g, L0_gnn_ln1_b, L0_gnn_ln2_g, L0_gnn_ln2_b, L0_gnn_wq, L0_gnn_bq, L0_gnn_wk, L0_gnn_bk, L0_gnn_wv, L0_gnn_bv, L0_gnn_wo, L0_gnn_bo, L0_gnn_w1, L0_gnn_b1, L0_gnn_w2, L0_gnn_b2, L1_gnn_Wq, L1_gnn_bq, L1_gnn_Wk, L1_gnn_bk, L1_gnn_Wc, L1_gnn_ln_g, L1_gnn_ln_b, L2_gnn_Wq, L2_gnn_Wk, L2_gnn_Wv, L2_gnn_Wo, L2_gnn_bo, L2_gnn_gamma, L2_gnn_beta, L3_gnn_Wd, L3_gnn_bd, L3_gnn_Wri, L3_gnn_bri, L3_gnn_Wrh, L3_gnn_brh, L3_gnn_Wzi, L3_gnn_bzi, L3_gnn_Wzh, L3_gnn_bzh, L3_gnn_Wni, L3_gnn_bni, L3_gnn_Wnh, L3_gnn_bnh, L3_gnn_gamma, L3_gnn_beta):
    import jax
    import jax.numpy as jnp

    def _L0_gnn_ref(x, adj_matrix, edge_attr_matrix, ln1_g, ln1_b, ln2_g, ln2_b, wq, bq, wk, bk, wv, bv, wo, bo, w1, b1, w2, b2):
        import jax, jax.numpy as jnp
        import numpy as np
        B, S, D, H = (2, 1024, 256, 8)
        HD = D // H
        EPS = 1e-05

        def _ln(x, g, b):
            mu = jnp.mean(x, axis=-1, keepdims=True)
            var = jnp.mean((x - mu) ** 2, axis=-1, keepdims=True)
            return (x - mu) * jax.lax.rsqrt(var + EPS) * g + b
        b, s, d = x.shape
        residual = x
        nx = _ln(x, ln1_g, ln1_b)
        q = (nx @ wq + bq).reshape(b, s, H, HD).transpose(0, 2, 1, 3)
        k = (nx @ wk + bk).reshape(b, s, H, HD).transpose(0, 2, 1, 3)
        v = (nx @ wv + bv).reshape(b, s, H, HD).transpose(0, 2, 1, 3)
        adjf = adj_matrix.astype(jnp.float32)
        bias = jnp.where(adj_matrix > 0, 0.1 * edge_attr_matrix * adjf, -jnp.inf)[:, None]
        scores = jnp.einsum('bhqd,bhkd->bhqk', q, k) / np.sqrt(HD) + bias
        attn = jax.nn.softmax(scores, axis=-1)
        out = jnp.einsum('bhqk,bhkd->bhqd', attn, v)
        out = out.transpose(0, 2, 1, 3).reshape(b, s, d)
        x1 = residual + (out @ wo + bo)
        n2 = _ln(x1, ln2_g, ln2_b)
        mlp = jax.nn.gelu(n2 @ w1 + b1, approximate=False) @ w2 + b2
        return x1 + mlp

    def _L1_gnn_ref(node_fts, rel_edges, Wq, bq, Wk, bk, Wc, ln_g, ln_b):
        import jax, jax.numpy as jnp
        import numpy as np
        B, N, E, FF, L = (8, 1024, 256, 128, 2)
        LN_EPS = 1e-05
        SCALE = float(np.sqrt(FF))

        def layer_norm(x, g, b):
            m = jnp.mean(x, axis=-1, keepdims=True)
            v = jnp.mean(jnp.square(x - m), axis=-1, keepdims=True)
            return (x - m) * jax.lax.rsqrt(v + LN_EPS) * g + b
        x = node_fts
        mask = rel_edges == 0
        for k in range(L):
            q = jnp.einsum('bnd,fd->bnf', x, Wq[k]) + bq[k]
            kk = jnp.einsum('bnd,fd->bnf', x, Wk[k]) + bk[k]
            scores = jnp.einsum('bof,bif->boi', q, kk) / SCALE
            scores = jnp.where(mask, -10000000000.0, scores)
            attn = jax.nn.softmax(scores, axis=2)
            attn = jnp.where(mask, 0.0, attn)
            ctx = jnp.einsum('boi,bid->bod', attn, x)
            ctx = jnp.einsum('bnd,ed->bne', ctx, Wc[k])
            x = layer_norm(x + ctx, ln_g[k], ln_b[k])
        return x

    def _L2_gnn_ref(x, adj, Wq, Wk, Wv, Wo, bo, gamma, beta):
        import jax, jax.numpy as jnp
        import numpy as np
        import math
        D = 256
        B, L = (8, 1024)
        EPS = 1e-05

        def layer_norm(y, gamma, beta):
            mu = jnp.mean(y, axis=-1, keepdims=True)
            var = jnp.mean(jnp.square(y - mu), axis=-1, keepdims=True)
            return (y - mu) * jax.lax.rsqrt(var + EPS) * gamma + beta
        d_out = Wq.shape[1]
        scale = 1.0 / math.sqrt(d_out)
        Q = x @ Wq
        K = x @ Wk
        V = x @ Wv
        sc = jnp.einsum('bld,bmd->blm', Q, K) * scale
        mask = adj == 0
        sc = jnp.where(mask, -jnp.inf, sc)
        all_inf = jnp.all(mask, axis=-1, keepdims=True)
        sc = jnp.where(all_inf, 0.0, sc)
        w = jax.nn.softmax(sc, axis=-1)
        out = jnp.einsum('blm,bmd->bld', w, V)
        y = x + out @ Wo + bo
        return layer_norm(y, gamma, beta)

    def _L3_gnn_ref(adj, relative_pos, hid, Wd, bd, Wri, bri, Wrh, brh, Wzi, bzi, Wzh, bzh, Wni, bni, Wnh, bnh, gamma, beta):
        import jax, jax.numpy as jnp
        import numpy as np
        B, N, H, D = (8, 512, 256, 4)
        EPS = 1e-08
        LN_EPS = 1e-05

        def _linear(x, W, b):
            return x @ W.T + b
        dt = hid.dtype
        labels = jnp.arange(1, D + 1, dtype=adj.dtype)
        mask = (adj[None] == labels[:, None, None, None]).astype(dt)
        weight = mask / (jnp.sum(mask, axis=-1, keepdims=True) + EPS)
        agg = jnp.einsum('dbmn,bnh->bmdh', weight, hid).reshape(hid.shape[0], hid.shape[1], D * H)
        out = jax.nn.relu(_linear(agg, Wd, bd))
        r = jax.nn.sigmoid(_linear(out, Wri, bri) + _linear(hid, Wrh, brh))
        z = jax.nn.sigmoid(_linear(out, Wzi, bzi) + _linear(hid, Wzh, bzh))
        n = jnp.tanh(_linear(out, Wni, bni) + r * _linear(hid, Wnh, bnh))
        out = (1.0 - z) * n + z * hid
        mu = jnp.mean(out, axis=-1, keepdims=True)
        var = jnp.var(out, axis=-1, keepdims=True)
        return (out - mu) / jnp.sqrt(var + LN_EPS) * gamma + beta
    x = _L0_gnn_ref(x, adj, adj, L0_gnn_ln1_g, L0_gnn_ln1_b, L0_gnn_ln2_g, L0_gnn_ln2_b, L0_gnn_wq, L0_gnn_bq, L0_gnn_wk, L0_gnn_bk, L0_gnn_wv, L0_gnn_bv, L0_gnn_wo, L0_gnn_bo, L0_gnn_w1, L0_gnn_b1, L0_gnn_w2, L0_gnn_b2)
    x = _L1_gnn_ref(x, adj, L1_gnn_Wq, L1_gnn_bq, L1_gnn_Wk, L1_gnn_bk, L1_gnn_Wc, L1_gnn_ln_g, L1_gnn_ln_b)
    x = _L2_gnn_ref(x, adj, L2_gnn_Wq, L2_gnn_Wk, L2_gnn_Wv, L2_gnn_Wo, L2_gnn_bo, L2_gnn_gamma, L2_gnn_beta)
    x = _L3_gnn_ref(adj, adj, x, L3_gnn_Wd, L3_gnn_bd, L3_gnn_Wri, L3_gnn_bri, L3_gnn_Wrh, L3_gnn_brh, L3_gnn_Wzi, L3_gnn_bzi, L3_gnn_Wzh, L3_gnn_bzh, L3_gnn_Wni, L3_gnn_bni, L3_gnn_Wnh, L3_gnn_bnh, L3_gnn_gamma, L3_gnn_beta)
    return x

_drawn_inputs = setup_inputs


def setup_inputs(seed=0):
    import zlib

    import numpy as np

    out = dict(_drawn_inputs(seed))
    spreads = {'L0_gnn_ln1_g': (1.0, 0.2),
     'L0_gnn_ln1_b': (0.0, 0.1),
     'L0_gnn_ln2_g': (1.0, 0.2),
     'L0_gnn_ln2_b': (0.0, 0.1),
     'L0_gnn_bq': (0.0, 0.1),
     'L0_gnn_bk': (0.0, 0.8),
     'L0_gnn_bv': (0.0, 0.1),
     'L0_gnn_bo': (0.0, 0.1),
     'L0_gnn_b1': (0.0, 0.1),
     'L0_gnn_b2': (0.0, 0.1),
     'L1_gnn_bq': (0.0, 0.8),
     'L1_gnn_bk': (0.0, 0.8),
     'L1_gnn_ln_g': (1.0, 0.2),
     'L1_gnn_ln_b': (0.0, 0.1),
     'L2_gnn_bo': (0.0, 0.1),
     'L2_gnn_gamma': (1.0, 0.2),
     'L2_gnn_beta': (0.0, 0.1),
     'L3_gnn_bd': (0.0, 0.1),
     'L3_gnn_bri': (0.0, 0.663),
     'L3_gnn_brh': (0.0, 0.696),
     'L3_gnn_bzi': (0.0, 0.1),
     'L3_gnn_bzh': (0.0, 0.1),
     'L3_gnn_bni': (0.0, 0.1),
     'L3_gnn_bnh': (0.0, 0.1),
     'L3_gnn_gamma': (1.0, 0.2),
     'L3_gnn_beta': (0.0, 0.1)}
    factors = {}
    for name, (base, spread) in spreads.items():
        noise = np.random.default_rng([zlib.crc32(name.encode()), seed]).standard_normal(out[name].shape)
        drawn = base * np.exp(spread * noise) if base else spread * noise
        out[name] = jnp.asarray(drawn.astype(out[name].dtype))
    for name, factor in factors.items():
        out[name] = (out[name] * factor).astype(out[name].dtype)
    return out
```

```python
from contextlib import ExitStack

import concourse.bass as bass
from concourse import mybir

P = 128
D = 256
HEADS, HD = 8, 32
QUADS = P // HD
C = D // P
PAIR = 2
TOK = PAIR * P
FF = 4 * D
FC = FF // P
LABELS = 4

F32 = mybir.dt.float32
F32R = mybir.dt.float32r
I32 = mybir.dt.int32
ALU = mybir.AluOpType
ACT = mybir.ActivationFunctionType
AX = mybir.AxisListType

MASKED = -1e30
LOWEST = -3.0e38
LN_EPS = 1e-5
COUNT_EPS = 1e-8



def split_product(pe, out, stationary, moving, start, stop):
    s_hi, s_lo = stationary
    m_hi, m_lo = moving
    pe.matmul(out, s_lo, m_hi, start=start, stop=False, skip_group_check=True)
    pe.matmul(out, s_hi, m_lo, start=False, stop=False, skip_group_check=True)
    return pe.matmul(out, s_hi, m_hi, start=False, stop=stop, skip_group_check=True)


def wait(eng, sem, value):
    if value is not None:
        eng.wait_ge(sem, value)


def apart(eng):
    eng.nop(nofuse=True)


class Turn:

    def __init__(self, group, now, before, four):
        self.group, self.now, self.before, self.four = group, now, before, four


def turns(eng, stages, groups, run, fourfold=None):
    def static(t):
        out = []
        for s in range(stages):
            g = t - s
            four = [4 * g + 1 + i for i in range(4)]
            out.append(Turn(g, g + 1, g if g > 0 else None, four) if 0 <= g < groups else None)
        return out

    first = stages
    for t in range(first):
        run(*static(t))
    with eng.Fori(first, groups) as t:
        at = [eng.snap(t + (1 - s)) if s != 1 else t for s in range(stages + 1)]
        four = [eng.snap(at[fourfold + 1] * 4 + (1 + i)) for i in range(4)] if fourfold is not None else None
        run(*[Turn(at[s + 1], at[s], at[s + 1], four if s == fourfold else None) for s in range(stages)])
    for t in range(groups, groups + stages - 1):
        run(*static(t))


def four_before(turn):
    return None if turn.before is None else turn.before * 4


def bytes_landed(value):
    return None if value is None else value * 16


def declare(ctx, nc):
    def sb(name, shape, dt=F32):
        return ctx.enter_context(nc.sbuf_tensor(name, shape, dt))

    def pair(name, shape):
        return sb(name + "_hi", shape, F32R), sb(name + "_lo", shape, F32R)

    def sems(names):
        got = {n: nc.alloc_semaphore(name=n) for n in names.split()}
        taken.extend(got.values())
        return got

    taken = []
    return sb, pair, sems, taken


def as_f32(ap):
    return ap.bitcast(F32)


def encoder_phase(nc, x, adj, w_dram, cols_dram, rows_dram, x2_dram):
    groups = x.shape[0] // PAIR
    x_g = x.rearrange("(g b) p d -> g p b d", b=PAIR)
    adj_g = adj.rearrange("(g b) p k -> g p b k", b=PAIR)
    x2_g = x2_dram.rearrange("(g b) p d -> g p b d", b=PAIR)
    scale = float(HD) ** -0.5
    bias_scale = 0.1 * float(HD) ** 0.5
    STAGES = 4
    CH = 2048
    n_w = w_dram.shape[1] // CH

    with ExitStack() as ctx:
        sb, pair, sems, taken = declare(ctx, nc)
        att_w = pair("att_w", [P, 4, C, D])
        w1 = pair("w1", [P, C, FF])
        w2 = pair("w2", [P, FC, D])
        flat = [[t[:, :].rearrange("p a c n -> p (a c n)") if len(t.shape) == 4 else
                 t[:, :].rearrange("p a n -> p (a n)") for t in w] for w in (att_w, w1, w2)]
        raw = sb("raw", [P, 2, CH])
        cols = sb("cols", [P, 2 * C + FC])
        rows = sb("rows", [P, 7, D])
        LN1_G, LN1_B, BV, BO, LN2_G, LN2_B, B2 = range(7)
        ident = sb("ident", [P, P])
        power = sb("power", [P, PAIR])

        x_in = sb("x_in", [P, PAIR, D])
        adj_in = sb("adj_in", [P, PAIR, P], I32)
        stats1 = sb("stats1", [P, PAIR, 6])
        mv1 = sb("mv1", [P, PAIR, 2])
        var1 = sb("var1", [P, PAIR])
        rstd1 = sb("rstd1", [P, PAIR])
        nx = sb("nx", [P, PAIR, D])
        masked = sb("masked", [P, PAIR, P])
        adj_f = sb("adj_f", [P, PAIR, P])
        scaled = sb("scaled", [P, PAIR, P])
        squares = sb("squares", [P, PAIR, P])
        edge_bias = sb("edge_bias", [P, PAIR, P])
        nxT = pair("nxT", [P, C, TOK])
        qT = pair("qT", [P, C, TOK])
        kT = pair("kT", [P, C, TOK])
        k_diag = pair("k_diag", [P, PAIR, C, QUADS, P])
        v_full = sb("v_full", [P, PAIR, D])
        v = pair("v", [P, PAIR, D])
        prob = sb("prob", [P, PAIR, HEADS, P])
        peak = sb("peak", [P, PAIR, HEADS])
        shift = sb("shift", [P, PAIR, HEADS])
        total = sb("total", [P, PAIR, HEADS])
        share = sb("share", [P, PAIR, HEADS])
        probT = pair("probT", [P, PAIR, C, QUADS, P])
        att_full = sb("att_full", [P, C, TOK])
        attT = pair("attT", [P, C, TOK])
        x_again = sb("x_again", [P, PAIR, D])
        x_bo = sb("x_bo", [P, PAIR, D])
        x1 = sb("x1", [P, PAIR, D])
        x1_b2 = sb("x1_b2", [P, PAIR, D])
        stats2 = sb("stats2", [P, PAIR, 6])
        mv2 = sb("mv2", [P, PAIR, 2])
        var2 = sb("var2", [P, PAIR])
        rstd2 = sb("rstd2", [P, PAIR])
        n2 = sb("n2", [P, PAIR, D])
        n2T = pair("n2T", [P, C, TOK])
        hid_full = [sb(f"hid_full{i}", [P, 2, TOK]) for i in range(2)]
        hidT = [pair(f"hidT{i}", [P, 2, TOK]) for i in range(2)]
        x2 = sb("x2", [P, PAIR, D])

        bank = [ctx.enter_context(nc.psum_tensor(f"bank{i}", [P, 512], F32)) for i in range(8)]

        load = sems("raw_landed0 raw_landed1 hi_done lo_done const_landed zeroed ident_zero ident_done")
        ev = sems(
            "x_landed adj_landed x_again_landed x2_stored "
            "stats1_done mv1_done var1_done rstd1_done z1_done g1_done nx_done "
            "masked_done squares_done scaled_done edge_bias_done "
            "nxT_psum nxT_hi nxT_lo q_psum k_psum v_psum q_hi k_hi q_lo k_lo diag_hi diag_lo "
            "v_full_done v_hi v_lo "
            "scores0 scores1 peak0 peak1 shift0 shift1 exp0 exp1 share0 share1 prob0 prob1 "
            "probT_psum0 probT_psum1 probT_hi0 probT_hi1 probT_lo0 probT_lo1 att_psum0 att_psum1 "
            "att_full0 att_full1 att_hi att_lo wo_psum x_bo_done x1_done x1_b2_done "
            "stats2_done mv2_done var2_done rstd2_done z2_done g2_done n2_done "
            "n2T_psum n2T_hi n2T_lo up0 up1 up2 up3 gelu0 gelu1 gelu2 gelu3 "
            "hid_hi0 hid_hi1 hid_hi2 hid_hi3 hid_lo0 hid_lo1 hid_lo2 hid_lo3 down0 down1 down2 down3 "
            "x2_done")
        block = ctx.enter_context(nc.Block())

        def b_(name, b):
            return ev[f"{name}{b}"]

        @block.sync
        def _(sp):
            sp.dma_start(cols[:, :], cols_dram).then_inc(load["const_landed"], 16)
            sp.dma_start(rows[:, :, :], rows_dram.partition_broadcast(P)).then_inc(load["const_landed"], 16)
            for n in range(n_w):
                if n >= 2:
                    sp.wait_ge(load["lo_done"], n - 1)
                sp.dma_start(raw[:, n % 2, :], w_dram[:, n * CH:(n + 1) * CH]).then_inc(load[f"raw_landed{n % 2}"], 16)

            def step(norm, proj, att, mlp):
                if norm:
                    wait(sp, ev["z1_done"], norm.before)
                    sp.dma_start(x_in[:, :, :], x_g[norm.group]).then_inc(ev["x_landed"], 16)
                if proj:
                    wait(sp, ev["scaled_done"], proj.before)
                    sp.dma_start(adj_in[:, :, :], adj_g[proj.group]).then_inc(ev["adj_landed"], 16)
                if att:
                    wait(sp, ev["x_bo_done"], att.before)
                    sp.dma_start(x_again[:, :, :], x_g[att.group]).then_inc(ev["x_again_landed"], 16)
                if mlp:
                    sp.wait_ge(ev["x2_done"], mlp.now)
                    sp.dma_start(x2_g[mlp.group], x2[:, :, :]).then_inc(ev["x2_stored"], 16)

            turns(sp, STAGES, groups, step)
            sp.wait_ge(ev["x2_stored"], 16 * groups)

        @block.gpsimd
        def _(pool):
            pool.memset(power[:, :], -0.5).then_inc(load["ident_zero"], 1)
            pool.memset(ident[:, :], 0.0).then_inc(load["ident_zero"], 1)
            pool.wait_ge(load["ident_zero"], 2)
            pool.affine_select(out=ident[:, :], in_=ident[:, :], compare_op=ALU.not_equal, fill=1.0, base=0,
                               pattern=[[-1, P]], channel_multiplier=1).then_inc(load["ident_done"], 1)
            pool.wait_ge(load["const_landed"], 32)

            def row(i):
                return rows[:, i:i + 1, :].broadcast_to([P, PAIR, D])

            def reciprocal_root(mv_done, mv, var, var_done, rstd, rstd_done, turn):
                pool.wait_ge(mv_done, turn.now)
                apart(pool)
                pool.tensor_scalar(var[:, :], mv[:, :, 1], LN_EPS, None, ALU.add).then_inc(var_done, 1)
                pool.wait_ge(var_done, turn.now)
                pool.tensor_tensor(rstd[:, :], var[:, :], power[:, :], ALU.pow).then_inc(rstd_done, 1)

            def step(norm, proj, att, mlp):
                if proj:
                    pool.wait_ge(ev["adj_landed"], bytes_landed(proj.now))
                    apart(pool)
                    pool.tensor_scalar(masked[:, :, :], adj_in[:, :, :], 0.0, MASKED, ALU.is_le,
                                       ALU.mult).then_inc(ev["masked_done"], 1)
                    pool.tensor_scalar(adj_f[:, :, :], adj_in[:, :, :], 1.0, None, ALU.mult)
                    pool.tensor_scalar(scaled[:, :, :], adj_in[:, :, :], bias_scale, None, ALU.mult).then_inc(ev["scaled_done"], 1)
                    pool.wait_ge(ev["scaled_done"], proj.now)
                    pool.tensor_tensor(squares[:, :, :], scaled[:, :, :], adj_f[:, :, :], ALU.mult).then_inc(ev["squares_done"], 1)
                    pool.wait_ge(ev["squares_done"], proj.now)
                    wait(pool, ev["peak1"], proj.before)
                    pool.tensor_tensor(edge_bias[:, :, :], squares[:, :, :], masked[:, :, :],
                                       ALU.add).then_inc(ev["edge_bias_done"], 1)
                if att:
                    pool.wait_ge(ev["x_again_landed"], bytes_landed(att.now))
                    wait(pool, ev["x1_done"], att.before)
                    pool.tensor_tensor(x_bo[:, :, :], x_again[:, :, :], row(BO), ALU.add).then_inc(ev["x_bo_done"], 1)
                if proj:
                    for b in range(PAIR):
                        pool.wait_ge(b_("share", b), proj.now)
                        pool.tensor_tensor(prob[:, b, :, :], prob[:, b, :, :],
                                           share[:, b, :].unsqueeze(2).broadcast_to([P, HEADS, P]),
                                           ALU.mult).then_inc(b_("prob", b), 1)
                if norm:
                    reciprocal_root(ev["mv1_done"], mv1, var1, ev["var1_done"], rstd1, ev["rstd1_done"], norm)
                    pool.wait_ge(ev["z1_done"], norm.now)
                    pool.tensor_tensor(nx[:, :, :], nx[:, :, :], row(LN1_G), ALU.mult).then_inc(ev["g1_done"], 1)
                    pool.wait_ge(ev["g1_done"], norm.now)
                    pool.tensor_tensor(nx[:, :, :], nx[:, :, :], row(LN1_B), ALU.add).then_inc(ev["nx_done"], 1)
                if att:
                    reciprocal_root(ev["mv2_done"], mv2, var2, ev["var2_done"], rstd2, ev["rstd2_done"], att)
                    pool.wait_ge(ev["z2_done"], att.now)
                    pool.tensor_tensor(n2[:, :, :], n2[:, :, :], row(LN2_G), ALU.mult).then_inc(ev["g2_done"], 1)
                    pool.wait_ge(ev["g2_done"], att.now)
                    pool.tensor_tensor(n2[:, :, :], n2[:, :, :], row(LN2_B), ALU.add).then_inc(ev["n2_done"], 1)
                    wait(pool, ev["x2_done"], att.before)
                    pool.tensor_tensor(x1_b2[:, :, :], x1[:, :, :], row(B2), ALU.add).then_inc(ev["x1_b2_done"], 1)
                if proj:
                    pool.wait_ge(ev["v_hi"], proj.now)
                    pool.tensor_tensor(v[1][:, :, :], v_full[:, :, :], as_f32(v[0][:, :, :]),
                                       ALU.subtract).then_inc(ev["v_lo"], 1)

            turns(pool, STAGES, groups, step)

        @block.scalar
        def _(act):
            for n in range(n_w):
                act.wait_ge(load[f"raw_landed{n % 2}"], 16 * (n // 2 + 1))
                act.activation(flat[n][0], raw[:, n % 2, :], ACT.Copy).then_inc(load["hi_done"], 1)
            act.wait_ge(load["const_landed"], 32)

            def step(norm, proj, att, mlp):
                def probT_hi(b):
                    act.wait_ge(b_("probT_psum", b), att.now)
                    wait(act, b_("att_psum", b), att.before)
                    for g in range(C):
                        last = act.activation(probT[0][:, b, g, :, :], bank[4 + g][:, :].rearrange("p (h k) -> p h k", h=QUADS), ACT.Copy)
                    last.then_inc(b_("probT_hi", b), 1)

                def att_full_(b):
                    act.wait_ge(b_("att_psum", b), att.now)
                    if b == 0:
                        wait(act, ev["att_lo"], att.before)
                    for g in range(C):
                        for j in range(QUADS):
                            rows_ = slice(HD * j, HD * (j + 1))
                            last = act.activation(att_full[rows_, g, b * P:(b + 1) * P],
                                                  bank[4 + g][rows_, j * P:(j + 1) * P], ACT.Copy)
                    last.then_inc(b_("att_full", b), 1)

                def exps(b):
                    act.wait_ge(b_("shift", b), proj.now)
                    for h in range(HEADS):
                        last = act.activation(prob[:, b, h, :], prob[:, b, h, :], ACT.Exp, bias=shift[:, b, h:h + 1],
                                              scale=scale, accum_out=total[:, b, h:h + 1])
                    last.then_inc(b_("exp", b), 1)

                def gelu(p):
                    act.wait_ge(b_("up", p), mlp.now)
                    if p >= 2:
                        act.wait_ge(b_("hid_lo", p - 2), mlp.now)
                    else:
                        wait(act, b_("hid_lo", p + 2), mlp.before)
                    for j in range(2):
                        last = act.activation(hid_full[p % 2][:, j, :], bank[6][:, j * TOK:(j + 1) * TOK], ACT.Gelu,
                                              bias=cols[:, 2 * C + 2 * p + j:2 * C + 2 * p + j + 1])
                    last.then_inc(b_("gelu", p), 1)

                if mlp:
                    act.wait_ge(ev["n2T_psum"], mlp.now)
                    wait(act, ev["up3"], mlp.before)
                    act.activation(n2T[0][:, :, :], bank[6][:, :].rearrange("p (c t) -> p c t", c=C), ACT.Copy).then_inc(ev["n2T_hi"], 1)
                if proj:
                    act.wait_ge(ev["nxT_psum"], proj.now)
                    wait(act, ev["v_psum"], proj.before)
                    act.activation(nxT[0][:, :, :], bank[0][:, :].rearrange("p (c t) -> p c t", c=C), ACT.Copy).then_inc(ev["nxT_hi"], 1)
                if att:
                    probT_hi(0)
                if proj:
                    for name, w, which, base in (("q", qT, 1, 0), ("k", kT, 2, C)):
                        act.wait_ge(ev[name + "_psum"], proj.now)
                        if name == "q":
                            wait(act, ev["scores1"], proj.before)
                        else:
                            wait(act, ev["diag_lo"], proj.before)
                        for m in range(C):
                            last = act.activation(w[0][:, m, :], bank[which][:, m * TOK:(m + 1) * TOK], ACT.Identity,
                                                  bias=cols[:, base + m:base + m + 1])
                        last.then_inc(ev[name + "_hi"], 1)
                    act.wait_ge(ev["k_hi"], proj.now)
                    wait(act, ev["scores1"], proj.before)
                    for j in range(QUADS):
                        rows_ = slice(HD * j, HD * (j + 1))
                        last = act.activation(k_diag[0][rows_, :, :, j, :],
                                              as_f32(kT[0][rows_, :, :]).rearrange("p c (b k) -> p b c k", b=PAIR), ACT.Copy)
                    last.then_inc(ev["diag_hi"], 1)
                if mlp:
                    gelu(0)
                if att:
                    probT_hi(1)
                if mlp:
                    gelu(1)
                if proj:
                    exps(0)
                if att:
                    att_full_(0)
                if mlp:
                    gelu(2)
                if proj:
                    exps(1)
                if att:
                    att_full_(1)
                if mlp:
                    gelu(3)
                if proj:
                    act.wait_ge(ev["v_full_done"], proj.now)
                    wait(act, ev["att_psum1"], proj.before)
                    act.activation(v[0][:, :, :], v_full[:, :, :], ACT.Copy).then_inc(ev["v_hi"], 1)

            turns(act, STAGES, groups, step)

        @block.vector
        def _(dve):
            for t in k_diag:
                last = dve.memset(as_f32(t[:, :, :, :, :]), 0.0)
            last.then_inc(load["zeroed"], 1)
            for n in range(n_w):
                dve.wait_ge(load["hi_done"], n + 1)
                dve.tensor_tensor(flat[n][1], raw[:, n % 2, :], as_f32(flat[n][0]), ALU.subtract).then_inc(load["lo_done"], 1)
            dve.wait_ge(load["const_landed"], 32)
            dve.wait_ge(load["zeroed"], 1)

            def norm_stats(src, stats, stats_done, mv, mv_done, turn):
                for b in range(PAIR):
                    last = dve.bn_stats(stats[:, b, :], src[:, b, :])
                last.then_inc(stats_done, 1)
                dve.wait_ge(stats_done, turn.now)
                apart(dve)
                for b in range(PAIR):
                    last = dve.bn_aggr(mv[:, b, :], stats[:, b, :])
                last.then_inc(mv_done, 1)

            def norm_apply(dst, src, mv, rstd, rstd_done, z_done, turned, turn):
                dve.wait_ge(rstd_done, turn.now)
                wait(dve, turned, turn.before)
                for b in range(PAIR):
                    last = dve.tensor_scalar(dst[:, b, :], src[:, b, :], mv[:, b, 0:1], rstd[:, b:b + 1],
                                             ALU.subtract, ALU.mult)
                last.then_inc(z_done, 1)

            def step(norm, proj, att, mlp):
                def probT_lo(b):
                    dve.wait_ge(b_("probT_hi", b), att.now)
                    for g in range(C):
                        last = dve.tensor_tensor(probT[1][:, b, g, :, :], bank[4 + g][:, :].rearrange("p (h k) -> p h k", h=QUADS),
                                                 as_f32(probT[0][:, b, g, :, :]), ALU.subtract)
                    last.then_inc(b_("probT_lo", b), 1)

                def peaks(b):
                    dve.wait_ge(b_("scores", b), proj.now)
                    if b == 0:
                        dve.wait_ge(ev["edge_bias_done"], proj.now)
                    wait(dve, b_("probT_psum", b), proj.before)
                    apart(dve)
                    for h in range(HEADS):
                        last = dve.tensor_tensor_reduce(prob[:, b, h, :], bank[2 * b + h // QUADS][:, (h % QUADS) * P:(h % QUADS + 1) * P],
                                                        edge_bias[:, b, :], 1.0, LOWEST, ALU.add, ALU.max, peak[:, b, h:h + 1])
                    last.then_inc(b_("peak", b), 1)
                    dve.wait_ge(b_("peak", b), proj.now)
                    dve.tensor_scalar(shift[:, b, :], peak[:, b, :], -scale, None, ALU.mult).then_inc(b_("shift", b), 1)

                def shares(b):
                    dve.wait_ge(b_("exp", b), proj.now)
                    dve.reciprocal(share[:, b, :], total[:, b, :]).then_inc(b_("share", b), 1)

                def hid_split(p):
                    hi, lo = hidT[p % 2]
                    dve.wait_ge(b_("gelu", p), mlp.now)
                    if p >= 2:
                        dve.wait_ge(b_("down", p - 2), mlp.now)
                    else:
                        wait(dve, b_("down", p + 2), mlp.before)
                    dve.tensor_copy(hi[:, :, :], hid_full[p % 2][:, :, :]).then_inc(b_("hid_hi", p), 1)
                    dve.wait_ge(b_("hid_hi", p), mlp.now)
                    dve.tensor_tensor(lo[:, :, :], hid_full[p % 2][:, :, :], as_f32(hi[:, :, :]), ALU.subtract).then_inc(b_("hid_lo", p), 1)

                if mlp:
                    dve.wait_ge(ev["n2T_hi"], mlp.now)
                    dve.tensor_tensor(n2T[1][:, :, :], bank[6][:, :].rearrange("p (c t) -> p c t", c=C), as_f32(n2T[0][:, :, :]),
                                      ALU.subtract).then_inc(ev["n2T_lo"], 1)
                if proj:
                    dve.wait_ge(ev["nxT_hi"], proj.now)
                    dve.tensor_tensor(nxT[1][:, :, :], bank[0][:, :].rearrange("p (c t) -> p c t", c=C), as_f32(nxT[0][:, :, :]),
                                      ALU.subtract).then_inc(ev["nxT_lo"], 1)
                if att:
                    probT_lo(0)
                if proj:
                    for name, w, which, base in (("q", qT, 1, 0), ("k", kT, 2, C)):
                        dve.wait_ge(ev[name + "_hi"], proj.now)
                        for m in range(C):
                            last = dve.scalar_tensor_tensor(out=w[1][:, m, :], in0=bank[which][:, m * TOK:(m + 1) * TOK],
                                                            scalar=cols[:, base + m:base + m + 1], in1=as_f32(w[0][:, m, :]),
                                                            op0=ALU.add, op1=ALU.subtract)
                        last.then_inc(ev[name + "_lo"], 1)
                    dve.wait_ge(ev["k_lo"], proj.now)
                    for j in range(QUADS):
                        rows_ = slice(HD * j, HD * (j + 1))
                        last = dve.tensor_copy(k_diag[1][rows_, :, :, j, :],
                                               as_f32(kT[1][rows_, :, :]).rearrange("p c (b k) -> p b c k", b=PAIR))
                    last.then_inc(ev["diag_lo"], 1)
                if att:
                    probT_lo(1)
                if mlp:
                    hid_split(0)
                if proj:
                    peaks(0)
                if mlp:
                    hid_split(1)
                if norm:
                    dve.wait_ge(ev["x_landed"], bytes_landed(norm.now))
                    norm_stats(x_in, stats1, ev["stats1_done"], mv1, ev["mv1_done"], norm)
                if proj:
                    peaks(1)
                    shares(0)
                if mlp:
                    hid_split(2)
                if proj:
                    shares(1)
                if att:
                    dve.wait_ge(ev["att_full1"], att.now)
                    dve.wait_ge(ev["att_full0"], att.now)
                    wait(dve, ev["wo_psum"], att.before)
                    dve.tensor_copy(attT[0][:, :, :], att_full[:, :, :]).then_inc(ev["att_hi"], 1)
                    dve.wait_ge(ev["att_hi"], att.now)
                    dve.tensor_tensor(attT[1][:, :, :], att_full[:, :, :], as_f32(attT[0][:, :, :]), ALU.subtract).then_inc(ev["att_lo"], 1)
                if mlp:
                    hid_split(3)
                if proj:
                    dve.wait_ge(ev["v_psum"], proj.now)
                    wait(dve, ev["v_lo"], proj.before)
                    dve.tensor_tensor(v_full[:, :, :], bank[3][:, :].rearrange("p (b d) -> p b d", b=PAIR),
                                      rows[:, BV:BV + 1, :].broadcast_to([P, PAIR, D]), ALU.add).then_inc(ev["v_full_done"], 1)
                if norm:
                    norm_apply(nx, x_in, mv1, rstd1, ev["rstd1_done"], ev["z1_done"], ev["nxT_psum"], norm)
                if mlp:
                    dve.wait_ge(ev["down3"], mlp.now)
                    dve.wait_ge(ev["x1_b2_done"], mlp.now)
                    wait(dve, ev["x2_stored"], bytes_landed(mlp.before))
                    dve.tensor_tensor(x2[:, :, :], bank[7][:, :].rearrange("p (b d) -> p b d", b=PAIR), x1_b2[:, :, :],
                                      ALU.add).then_inc(ev["x2_done"], 1)
                if att:
                    dve.wait_ge(ev["wo_psum"], att.now)
                    dve.wait_ge(ev["x_bo_done"], att.now)
                    wait(dve, ev["x1_b2_done"], att.before)
                    dve.tensor_tensor(x1[:, :, :], bank[4][:, :].rearrange("p (b d) -> p b d", b=PAIR), x_bo[:, :, :],
                                      ALU.add).then_inc(ev["x1_done"], 1)
                    dve.wait_ge(ev["x1_done"], att.now)
                    norm_stats(x1, stats2, ev["stats2_done"], mv2, ev["mv2_done"], att)
                    norm_apply(n2, x1, mv2, rstd2, ev["rstd2_done"], ev["z2_done"], ev["n2T_psum"], att)

            turns(dve, STAGES, groups, step)

        @block.tensor
        def _(pe):
            pe.wait_ge(load["ident_done"], 1)
            pe.wait_ge(load["lo_done"], n_w)

            def transposes(out, src):
                for c in range(C):
                    for b in range(PAIR):
                        last = pe.transpose(out[:, c * TOK + b * P:c * TOK + (b + 1) * P], src[:, b, c * P:(c + 1) * P], ident[:, :])
                return last

            def feature_rows(out, w, which, actT):
                for m in range(C):
                    for c in range(C):
                        last = split_product(pe, out[:, m * TOK:(m + 1) * TOK], [t[:, which, c, m * P:(m + 1) * P] for t in w],
                                             [t[:, c, :] for t in actT], c == 0, c == C - 1)
                return last

            def token_rows(out, w, which, actT):
                for b in range(PAIR):
                    for c in range(C):
                        last = split_product(pe, out[:, b * D:(b + 1) * D], [t[:, c, b * P:(b + 1) * P] for t in actT],
                                             [t[:, which, c, :] for t in w], c == 0, c == C - 1)
                return last

            def step(norm, proj, att, mlp):
                def probs_turned(b):
                    pe.wait_ge(b_("prob", b), att.now)
                    if b == 0:
                        wait(pe, ev["x1_done"], att.before)
                        wait(pe, ev["att_full1"], att.before)
                    else:
                        pe.wait_ge(ev["probT_lo0"], att.now)
                    for h in range(HEADS):
                        last = pe.transpose(bank[4 + h // QUADS][:, (h % QUADS) * P:(h % QUADS + 1) * P], prob[:, b, h, :], ident[:, :])
                    last.then_inc(b_("probT_psum", b), 1)

                def attend(b):
                    if b == 0:
                        pe.wait_ge(ev["probT_lo1"], att.now)
                        pe.wait_ge(ev["probT_lo0"], att.now)
                        pe.wait_ge(ev["v_lo"], att.now)
                    else:
                        pe.wait_ge(ev["att_full0"], att.now)
                    for g in range(C):
                        last = split_product(pe, bank[4 + g][:, :], [t[:, b, g * P:(g + 1) * P] for t in v],
                                             [t[:, b, g, :, :].rearrange("p h k -> p (h k)") for t in probT], True, True)
                    last.then_inc(b_("att_psum", b), 1)

                def scores(b):
                    if b == 0:
                        pe.wait_ge(ev["q_lo"], proj.now)
                        pe.wait_ge(ev["diag_hi"], proj.now)
                        pe.wait_ge(ev["diag_lo"], proj.now)
                    else:
                        wait(pe, ev["v_full_done"], proj.before)
                    for g in range(C):
                        last = split_product(pe, bank[2 * b + g][:, :], [t[:, g, b * P:(b + 1) * P] for t in qT],
                                             [t[:, b, g, :, :].rearrange("p h k -> p (h k)") for t in k_diag], True, True)
                    last.then_inc(b_("scores", b), 1)

                def up(p):
                    if p == 0:
                        pe.wait_ge(ev["n2T_lo"], mlp.now)
                    else:
                        pe.wait_ge(b_("gelu", p - 1), mlp.now)
                    for j in range(2):
                        f = (2 * p + j) * P
                        for c in range(C):
                            last = split_product(pe, bank[6][:, j * TOK:(j + 1) * TOK], [t[:, c, f:f + P] for t in w1],
                                                 [t[:, c, :] for t in n2T], c == 0, c == C - 1)
                    last.then_inc(b_("up", p), 1)

                def down(p):
                    pe.wait_ge(b_("hid_lo", p), mlp.now)
                    if p == 0:
                        wait(pe, ev["x2_done"], mlp.before)
                    for j in range(2):
                        for b in range(PAIR):
                            last = split_product(pe, bank[7][:, b * D:(b + 1) * D], [t[:, j, b * P:(b + 1) * P] for t in hidT[p % 2]],
                                                 [t[:, 2 * p + j, :] for t in w2], p == 0 and j == 0 and b == 0, p == 3 and j == 1)
                    last.then_inc(b_("down", p), 1)

                if mlp:
                    pe.wait_ge(ev["n2_done"], mlp.now)
                    wait(pe, ev["gelu3"], mlp.before)
                    transposes(bank[6], n2).then_inc(ev["n2T_psum"], 1)
                if proj:
                    pe.wait_ge(ev["nx_done"], proj.now)
                    wait(pe, ev["peak0"], proj.before)
                    transposes(bank[0], nx).then_inc(ev["nxT_psum"], 1)
                if att:
                    probs_turned(0)
                if mlp:
                    up(0)
                if proj:
                    pe.wait_ge(ev["nxT_lo"], proj.now)
                    feature_rows(bank[1], att_w, 0, nxT).then_inc(ev["q_psum"], 1)
                    wait(pe, ev["peak1"], proj.before)
                    feature_rows(bank[2], att_w, 1, nxT).then_inc(ev["k_psum"], 1)
                if att:
                    probs_turned(1)
                if mlp:
                    up(1)
                    down(0)
                if att:
                    attend(0)
                if proj:
                    scores(0)
                if mlp:
                    up(2)
                    down(1)
                if att:
                    attend(1)
                if proj:
                    scores(1)
                if mlp:
                    up(3)
                    down(2)
                if proj:
                    pe.wait_ge(ev["peak1"], proj.now)
                    token_rows(bank[3], att_w, 2, nxT).then_inc(ev["v_psum"], 1)
                if mlp:
                    down(3)
                if att:
                    pe.wait_ge(ev["att_lo"], att.now)
                    token_rows(bank[4], att_w, 3, attT).then_inc(ev["wo_psum"], 1)

            turns(pe, STAGES, groups, step)
    return taken


def graph_phase(nc, x2_dram, adj, adjT, w_dram, cols_dram, rows_dram, out_dram):
    groups = x2_dram.shape[0] // PAIR
    x2_g = x2_dram.rearrange("(g b) p d -> g p b d", b=PAIR)
    adj_g = adj.rearrange("(g b) p k -> g p b k", b=PAIR)
    adjT_g = adjT.rearrange("(g b) k p -> g k b p", b=PAIR)
    out_g = out_dram.rearrange("(g b) p d -> g p b d", b=PAIR)
    STAGES = 4
    CH = 2048
    W1, W2, WD, WG = 0, 1024 * 2, 2048 * 2, 2048 * 3
    score_scale = [float(P) ** -0.5, float(P) ** -0.5, float(D) ** -0.5]

    with ExitStack() as ctx:
        sb, pair, sems, taken = declare(ctx, nc)
        w1 = pair("w1_", [P, 2, 1024])
        w2 = pair("w2_", [P, 2, C, D])
        wd = pair("wd", [P, C, LABELS * D])
        wg = pair("wg", [P, 6, C, D])
        raw = sb("raw_", [P, 2, CH])
        cols = sb("cols_", [P, 4 + 12])
        gate_b = sb("gate_b", [P, 2, C])
        gate_sum = sb("gate_sum", [P, 2, C])
        rows = sb("rows_", [P, 10, D])
        NORM_G, NORM_B, BO, BD = [0, 2, 5, 8], [1, 3, 6, 9], 4, 7
        ident = sb("ident_", [P, P])
        power = sb("power_", [P, PAIR])

        class Attention:

            def __init__(self, n):
                def own(name, shape, dt=F32):
                    return sb(f"{name}_{n}", shape, dt)
                self.n = n
                self.adj = own("adj", [P, PAIR, P], I32)
                self.mask = own("mask", [P, PAIR, P])
                self.any = own("any", [P, PAIR])
                self.keep = own("keep", [P, PAIR])
                self.xT = pair(f"xT_{n}", [P, C, TOK])
                self.xT_full = own("xT_full", [P, C, TOK]) if n == 2 else None
                self.q = own("q", [P, C, TOK])
                self.y = pair(f"y_{n}", [P, PAIR, D])
                self.prob = own("prob", [P, PAIR, P])
                self.peak = own("peak", [P, PAIR])
                self.shift = own("shift", [P, PAIR])
                self.total = own("total", [P, PAIR])
                self.inv = own("inv", [P, PAIR])
                self.share = own("share", [P, PAIR]) if n < 2 else self.inv
                self.probT = pair(f"probT_{n}", [P, PAIR, P])
                self.xr = own("xr", [P, PAIR, D])
                self.stats = own("stats", [P, PAIR, 6])
                self.mv = own("mv", [P, PAIR, 2])
                self.var = own("var", [P, PAIR])
                self.rstd = own("rstd", [P, PAIR])
                self.ev = sems(" ".join(f"{e}_{n}" for e in self.EVENTS.split()
                                        if n < 2 or e not in ("any_done", "keep_done", "share")))
                self.base = 2 * n

            EVENTS = ("adj_landed mask_done any_done keep_done xT_psum xT_hi xT_lo q_psum y_psum q_done y_hi y_lo "
                      "scores peak shift exp inv share probT_psum probT_hi probT_lo ctx_psum xr_done stats mv var rstd "
                      "z g x_done")

            def __getitem__(self, name):
                if name == "share" and self.n == 2:
                    name = "inv"
                return self.ev[f"{name}_{self.n}"]

        x_in = sb("x_in_", [P, PAIR, D])
        x = [x_in] + [sb(f"x_{n}", [P, PAIR, D]) for n in range(1, 4)]
        A = [Attention(n) for n in range(3)]
        x_bo = sb("x_bo_", [P, PAIR, D])

        adjT_in = sb("adjT_in", [P, PAIR, P], I32)
        adj_in = sb("adj_in_", [P, PAIR, P], I32)
        maskT = sb("maskT", [P, PAIR, LABELS, P], F32R)
        mask_m = sb("mask_m", [P, PAIR, LABELS, P])
        count = sb("count", [P, PAIR, LABELS])
        count_eps = sb("count_eps", [P, PAIR, LABELS])
        mean_w = sb("mean_w", [P, PAIR, LABELS])
        hT_full = sb("hT_full", [P, C, TOK])
        hT = pair("hT", [P, C, TOK])
        Y = pair("Y", [P, PAIR, LABELS * D])
        acc = sb("acc", [P, PAIR, D])
        acc2 = sb("acc2", [P, PAIR, D])
        oT = pair("oT", [P, C, TOK])
        r_gate = sb("r_gate", [P, C, TOK])
        z_gate = sb("z_gate", [P, C, TOK])
        hn = sb("hn", [P, C, TOK])
        pre = sb("pre", [P, C, TOK])
        n_gate = sb("n_gate", [P, C, TOK])
        diff, newT = hn, pre
        stats3 = sb("stats3", [P, PAIR, 6])
        mv3 = sb("mv3", [P, PAIR, 2])
        var3 = sb("var3", [P, PAIR])
        rstd3 = sb("rstd3", [P, PAIR])
        result = sb("result", [P, PAIR, D])

        bank = [ctx.enter_context(nc.psum_tensor(f"gbank{i}", [P, 512], F32)) for i in range(8)]
        load = sems("graw_landed0 graw_landed1 ghi_done glo_done gconst_landed setup_done fused_psum")
        ev = sems("gx_landed bo_done label_adj_landed label_adjT_landed maskT_done mask_m_done count_done count_eps_done mean_w_done "
                  "hT_psum hT_full hT_hi hT_lo "
                  "Y_psum Y_hi Y_lo sums half_mean mean "
                  "oT_psum oT_hi oT_lo r_psum r_tanh r_done z_psum z_tanh z_done nh_psum hn_done ni_psum pre_done "
                  "n_done diff_done zdiff_done newT_done new_psum stats3 mv3 var3 rstd3 z3 g3 result_done stored")
        block = ctx.enter_context(nc.Block())

        def halves(ap):
            return ap.rearrange("p (c t) -> p c t", c=2)

        @block.sync
        def _(sp):
            sp.dma_start(cols[:, :], cols_dram).then_inc(load["gconst_landed"], 16)
            sp.dma_start(rows[:, :, :], rows_dram.partition_broadcast(P)).then_inc(load["gconst_landed"], 16)
            for n in range(5):
                if n >= 2:
                    sp.wait_ge(load["glo_done"], n - 1)
                if n == 3:
                    sp.wait_ge(load["fused_psum"], 2)
                width = min(CH, w_dram.shape[1] - n * CH)
                sp.dma_start(raw[:, n % 2, 0:width], w_dram[:, n * CH:n * CH + width]).then_inc(load[f"graw_landed{n % 2}"], 16)

            def step(*stage):
                for n in range(3):
                    if stage[n]:
                        wait(sp, A[n]["mask_done"], stage[n].before)
                        sp.dma_start(A[n].adj[:, :, :], adj_g[stage[n].group]).then_inc(A[n]["adj_landed"], 16)
                if stage[0]:
                    wait(sp, A[0]["xr_done"], stage[0].before)
                    sp.dma_start(x_in[:, :, :], x2_g[stage[0].group]).then_inc(ev["gx_landed"], 16)
                gru = stage[3]
                if gru:
                    wait(sp, ev["maskT_done"], gru.before)
                    sp.dma_start(adjT_in[:, :, :], adjT_g[gru.group]).then_inc(ev["label_adjT_landed"], 16)
                    wait(sp, ev["mask_m_done"], gru.before)
                    sp.dma_start(adj_in[:, :, :], adj_g[gru.group]).then_inc(ev["label_adj_landed"], 16)
                    sp.wait_ge(ev["result_done"], gru.now)
                    sp.dma_start(out_g[gru.group], result[:, :, :]).then_inc(ev["stored"], 16)

            turns(sp, STAGES, groups, step)
            sp.wait_ge(ev["stored"], 16 * groups)

        @block.gpsimd
        def _(pool):
            pool.memset(power[:, :], -0.5).then_inc(load["setup_done"], 1)
            pool.memset(ident[:, :], 0.0).then_inc(load["setup_done"], 1)
            pool.wait_ge(load["setup_done"], 2)
            pool.affine_select(out=ident[:, :], in_=ident[:, :], compare_op=ALU.not_equal, fill=1.0, base=0,
                               pattern=[[-1, P]], channel_multiplier=1).then_inc(load["setup_done"], 1)
            pool.wait_ge(load["gconst_landed"], 32)
            for i in range(2):
                a = 4 + 4 * i
                last = pool.tensor_tensor(gate_sum[:, i, :], cols[:, a:a + C], cols[:, a + C:a + 2 * C], ALU.add)
            last.then_inc(load["setup_done"], 1)
            pool.wait_ge(load["setup_done"], 4)
            pool.tensor_scalar(gate_b[:, :, :], gate_sum[:, :, :], 0.5, None, ALU.mult).then_inc(load["setup_done"], 1)

            def row(i):
                return rows[:, i:i + 1, :].broadcast_to([P, PAIR, D])

            def mask(a, turn):
                pool.wait_ge(a["adj_landed"], bytes_landed(turn.now))
                wait(pool, a["peak"], turn.before)
                apart(pool)
                pool.tensor_scalar(a.mask[:, :, :], a.adj[:, :, :], 0.0, MASKED, ALU.is_equal, ALU.mult).then_inc(a["mask_done"], 1)

            def norm(dst, mv_done, mv, var_done, var, rstd_done, rstd, z, g, done, n, turn):
                pool.wait_ge(mv_done, turn.now)
                apart(pool)
                pool.tensor_scalar(var[:, :], mv[:, :, 1], LN_EPS, None, ALU.add).then_inc(var_done, 1)
                pool.wait_ge(var_done, turn.now)
                pool.tensor_tensor(rstd[:, :], var[:, :], power[:, :], ALU.pow).then_inc(rstd_done, 1)
                pool.wait_ge(z, turn.now)
                pool.tensor_tensor(dst[:, :, :], dst[:, :, :], row(NORM_G[n]), ALU.mult).then_inc(g, 1)
                pool.wait_ge(g, turn.now)
                pool.tensor_tensor(dst[:, :, :], dst[:, :, :], row(NORM_B[n]), ALU.add).then_inc(done, 1)

            def step(*stage):
                gru = stage[3]
                for n in range(3):
                    if stage[n]:
                        mask(A[n], stage[n])
                if stage[2]:
                    pool.wait_ge(A[1]["x_done"], stage[2].now)
                    wait(pool, A[2]["xr_done"], stage[2].before)
                    pool.tensor_tensor(x_bo[:, :, :], x[2][:, :, :], row(BO), ALU.add).then_inc(ev["bo_done"], 1)
                if gru:
                    pool.wait_ge(ev["label_adjT_landed"], bytes_landed(gru.now))
                    wait(pool, ev["sums"], four_before(gru))
                    apart(pool)
                    for d in range(LABELS):
                        last = pool.tensor_scalar(maskT[:, :, d, :], adjT_in[:, :, :], float(d + 1), None, ALU.is_equal)
                    last.then_inc(ev["maskT_done"], 1)
                    pool.wait_ge(ev["label_adj_landed"], bytes_landed(gru.now))
                    wait(pool, ev["count_done"], gru.before)
                    apart(pool)
                    for d in range(LABELS):
                        last = pool.tensor_scalar(mask_m[:, :, d, :], adj_in[:, :, :], float(d + 1), None, ALU.is_equal)
                    last.then_inc(ev["mask_m_done"], 1)
                    pool.wait_ge(ev["r_tanh"], gru.now)
                    apart(pool)
                    pool.tensor_scalar(r_gate[:, :, :], r_gate[:, :, :], 0.5, 0.5, ALU.mult, ALU.add).then_inc(ev["r_done"], 1)
                    pool.wait_ge(ev["z_tanh"], gru.now)
                    apart(pool)
                    pool.tensor_scalar(z_gate[:, :, :], z_gate[:, :, :], 0.5, 0.5, ALU.mult, ALU.add).then_inc(ev["z_done"], 1)
                for n in (2, 1, 0):
                    a = A[n]
                    if stage[n]:
                        norm(x[n + 1], a["mv"], a.mv, a["var"], a.var, a["rstd"], a.rstd, a["z"], a["g"], a["x_done"], n, stage[n])
                if gru:
                    norm(result, ev["mv3"], mv3, ev["var3"], var3, ev["rstd3"], rstd3, ev["z3"], ev["g3"], ev["result_done"], 3, gru)

            turns(pool, STAGES, groups, step, fourfold=3)

        def flat(t):
            return t.rearrange("p a c n -> p (a c n)") if len(t.shape) == 4 else t.rearrange("p a n -> p (a n)")

        split_to = [(0, [flat(t[:, :, :]) for t in w1]), (2, [flat(t[:, :, :]) for t in wd]),
                    (3, [flat(t[:, :, :, :])[:, 0:CH] for t in wg]), (4, [flat(t[:, :, :, :])[:, CH:6 * C * D] for t in wg])]

        @block.scalar
        def _(act):
            for i, (n, w) in enumerate(split_to):
                act.wait_ge(load[f"graw_landed{n % 2}"], 16 * (n // 2 + 1))
                act.activation(w[0], raw[:, n % 2, 0:w[0].shape[1]], ACT.Copy).then_inc(load["ghi_done"], 1)
                if i == 0:
                    for k in range(2):
                        act.wait_ge(load["fused_psum"], k + 1)
                        act.activation(w2[0][:, k, :, :], halves(bank[k][:, :]), ACT.Copy).then_inc(load["ghi_done"], 1)
            act.wait_ge(load["gconst_landed"], 32)
            act.wait_ge(load["setup_done"], 5)

            def turned(a, turn):
                act.wait_ge(a["xT_psum"], turn.now)
                if a.n == 2:
                    wait(act, a["scores"], turn.before)
                    act.activation(a.xT_full[:, :, :], halves(bank[a.base][:, :]), ACT.Copy)
                wait(act, a["y_psum"], turn.before)
                act.activation(a.xT[0][:, :, :], halves(bank[a.base][:, :]), ACT.Copy).then_inc(a["xT_hi"], 1)

            def projected(a, turn):
                act.wait_ge(a["q_psum"], turn.now)
                wait(act, a["scores"], turn.before)
                if a.n < 2:
                    for i in range(2):
                        last = act.activation(a.q[:, i, :], bank[a.base][:, i * TOK:(i + 1) * TOK], ACT.Identity,
                                              bias=cols[:, 2 * a.n + i:2 * a.n + i + 1])
                else:
                    last = act.activation(a.q[:, :, :], halves(bank[a.base][:, :]), ACT.Copy)
                last.then_inc(a["q_done"], 1)
                act.wait_ge(a["y_psum"], turn.now)
                wait(act, a["ctx_psum"], turn.before)
                act.activation(a.y[0][:, :, :], halves(bank[a.base + 1][:, :]), ACT.Copy).then_inc(a["y_hi"], 1)

            def exps(a, turn):
                act.wait_ge(a["shift"], turn.now)
                for b in range(PAIR):
                    last = act.activation(a.prob[:, b, :], a.prob[:, b, :], ACT.Exp, bias=a.shift[:, b:b + 1],
                                          scale=score_scale[a.n], accum_out=a.total[:, b:b + 1])
                last.then_inc(a["exp"], 1)

            def probs_turned(a, turn):
                act.wait_ge(a["probT_psum"], turn.now)
                wait(act, a["ctx_psum"], turn.before)
                act.activation(a.probT[0][:, :, :], halves(bank[a.base + 1][:, 0:PAIR * P]), ACT.Copy).then_inc(a["probT_hi"], 1)

            def step(*stage):
                gru = stage[3]

                def each(f):
                    for n in (2, 1, 0):
                        if stage[n]:
                            f(A[n], stage[n])

                def Y_hi(i):
                    b, half = i // 2, i % 2
                    act.wait_ge(ev["Y_psum"], gru.four[i])
                    if i == 0:
                        wait(act, ev["sums"], four_before(gru))
                    act.activation(Y[0][:, b, half * 512:(half + 1) * 512], bank[6 + i % 2][:, :], ACT.Copy).then_inc(ev["Y_hi"], 1)

                def tanh(dst, psum, scale, bias, done):
                    for m in range(C):
                        last = act.activation(dst[:, m, :], psum[:, m, :], ACT.Tanh, bias=bias[:, m:m + 1], scale=scale)
                    last.then_inc(done, 1)

                if gru:
                    act.wait_ge(ev["hT_psum"], gru.now)
                    wait(act, ev["diff_done"], gru.before)
                    act.activation(hT_full[:, :, :], halves(bank[6][:, :]), ACT.Copy).then_inc(ev["hT_full"], 1)
                    wait(act, ev["nh_psum"], gru.before)
                    wait(act, ev["z_psum"], gru.before)
                    act.activation(hT[0][:, :, :], halves(bank[6][:, :]), ACT.Copy).then_inc(ev["hT_hi"], 1)
                each(turned)
                if gru:
                    Y_hi(0)
                    Y_hi(1)
                each(projected)
                if gru:
                    Y_hi(2)
                    Y_hi(3)
                each(exps)
                if gru:
                    act.wait_ge(ev["oT_psum"], gru.now)
                    wait(act, ev["ni_psum"], gru.before)
                    act.activation(oT[0][:, :, :], halves(bank[6][:, :]), ACT.Relu).then_inc(ev["oT_hi"], 1)
                each(probs_turned)
                if gru:
                    act.wait_ge(ev["r_psum"], gru.now)
                    tanh(r_gate, halves(bank[7][:, :]), 0.5, gate_b[:, 0, :], ev["r_tanh"])
                    act.wait_ge(ev["z_psum"], gru.now)
                    tanh(z_gate, halves(bank[7][:, :]), 0.5, gate_b[:, 1, :], ev["z_tanh"])
                    act.wait_ge(ev["pre_done"], gru.now)
                    tanh(n_gate, pre, 1.0, cols[:, 12:14], ev["n_done"])

            turns(act, STAGES, groups, step, fourfold=3)

        @block.vector
        def _(dve):
            for i, (n, w) in enumerate(split_to):
                dve.wait_ge(load["ghi_done"], i + 1 if i == 0 else i + 3)
                dve.tensor_tensor(w[1], raw[:, n % 2, 0:w[0].shape[1]], as_f32(w[0]), ALU.subtract).then_inc(load["glo_done"], 1)
                if i == 0:
                    for k in range(2):
                        dve.wait_ge(load["ghi_done"], k + 2)
                        last = dve.tensor_tensor(w2[1][:, k, :, :], halves(bank[k][:, :]), as_f32(w2[0][:, k, :, :]), ALU.subtract)
                    last.then_inc(load["glo_done"], 1)
            dve.wait_ge(load["gconst_landed"], 32)

            def norm(dst, src, stats, stats_done, mv, mv_done, rstd, rstd_done, z_done, free, turn):
                for b in range(PAIR):
                    last = dve.bn_stats(stats[:, b, :], src[:, b, :])
                last.then_inc(stats_done, 1)
                dve.wait_ge(stats_done, turn.now)
                apart(dve)
                for b in range(PAIR):
                    last = dve.bn_aggr(mv[:, b, :], stats[:, b, :])
                last.then_inc(mv_done, 1)
                dve.wait_ge(rstd_done, turn.now)
                for sem, value in free:
                    wait(dve, sem, value)
                for b in range(PAIR):
                    last = dve.tensor_scalar(dst[:, b, :], src[:, b, :], mv[:, b, 0:1], rstd[:, b:b + 1],
                                             ALU.subtract, ALU.mult)
                last.then_inc(z_done, 1)

            def turned(a, turn):
                dve.wait_ge(a["xT_hi"], turn.now)
                dve.tensor_tensor(a.xT[1][:, :, :], halves(bank[a.base][:, :]), as_f32(a.xT[0][:, :, :]),
                                  ALU.subtract).then_inc(a["xT_lo"], 1)

            def keeps(a, turn):
                dve.wait_ge(a["mask_done"], turn.now)
                dve.tensor_reduce(a.any[:, :], a.mask[:, :, :], AX.X, ALU.max).then_inc(a["any_done"], 1)
                dve.wait_ge(a["any_done"], turn.now)
                dve.tensor_scalar(a.keep[:, :], a.any[:, :], -1.0, None, ALU.is_gt).then_inc(a["keep_done"], 1)

            def projected(a, turn):
                dve.wait_ge(a["y_hi"], turn.now)
                dve.tensor_tensor(a.y[1][:, :, :], halves(bank[a.base + 1][:, :]), as_f32(a.y[0][:, :, :]),
                                  ALU.subtract).then_inc(a["y_lo"], 1)

            def peaks(a, turn):
                dve.wait_ge(a["scores"], turn.now)
                dve.wait_ge(a["mask_done"], turn.now)
                wait(dve, a["probT_psum"], turn.before)
                apart(dve)
                for b in range(PAIR):
                    last = dve.tensor_tensor_reduce(a.prob[:, b, :], bank[a.base][:, b * P:(b + 1) * P], a.mask[:, b, :],
                                                    1.0, LOWEST, ALU.add, ALU.max, a.peak[:, b:b + 1])
                last.then_inc(a["peak"], 1)
                dve.wait_ge(a["peak"], turn.now)
                dve.tensor_scalar(a.shift[:, :], a.peak[:, :], -score_scale[a.n], None, ALU.mult).then_inc(a["shift"], 1)

            def shares(a, turn):
                dve.wait_ge(a["exp"], turn.now)
                dve.reciprocal(a.inv[:, :], a.total[:, :]).then_inc(a["inv"], 1)
                dve.wait_ge(a["inv"], turn.now)
                if a.n < 2:
                    dve.wait_ge(a["keep_done"], turn.now)
                    dve.tensor_tensor(a.share[:, :], a.inv[:, :], a.keep[:, :], ALU.mult).then_inc(a["share"], 1)

            def probs_turned(a, turn):
                dve.wait_ge(a["probT_hi"], turn.now)
                dve.tensor_tensor(a.probT[1][:, :, :], halves(bank[a.base + 1][:, 0:PAIR * P]), as_f32(a.probT[0][:, :, :]),
                                  ALU.subtract).then_inc(a["probT_lo"], 1)

            def attended(a, turn):
                dve.wait_ge(a["ctx_psum"], turn.now)
                dve.wait_ge(a["share"], turn.now)
                res = x_bo if a.n == 2 else x[a.n]
                if a.n == 2:
                    dve.wait_ge(ev["bo_done"], turn.now)
                for b in range(PAIR):
                    last = dve.scalar_tensor_tensor(out=a.xr[:, b, :], in0=bank[a.base][:, b * D:(b + 1) * D],
                                                    scalar=a.share[:, b:b + 1], in1=res[:, b, :], op0=ALU.mult, op1=ALU.add)
                last.then_inc(a["xr_done"], 1)
                dve.wait_ge(a["xr_done"], turn.now)
                if a.n == 0:
                    free = [(A[1]["xT_psum"], turn.before), (A[1]["xr_done"], turn.before)]
                elif a.n == 1:
                    free = [(A[2]["xT_psum"], turn.before), (ev["bo_done"], turn.before)]
                else:
                    free = [(ev["hT_psum"], turn.before)]
                norm(x[a.n + 1], a.xr, a.stats, a["stats"], a.mv, a["mv"], a.rstd, a["rstd"], a["z"], free, turn)

            def step(*stage):
                gru = stage[3]

                def each(f, ns=(2, 1, 0)):
                    for n in ns:
                        if stage[n]:
                            f(A[n], stage[n])

                def Y_lo(i):
                    b, half = i // 2, i % 2
                    dve.wait_ge(ev["Y_hi"], gru.four[i])
                    dve.tensor_tensor(Y[1][:, b, half * 512:(half + 1) * 512], bank[6 + i % 2][:, :],
                                      as_f32(Y[0][:, b, half * 512:(half + 1) * 512]), ALU.subtract).then_inc(ev["Y_lo"], 1)

                def mean(i):
                    b, half = i // 2, i % 2
                    dve.wait_ge(ev["sums"], gru.four[i])
                    d = 2 * half
                    start = rows[:, BD, :] if half == 0 else acc[:, b, :]
                    if half == 1:
                        dve.wait_ge(ev["mean"], gru.four[i - 1])
                    dve.scalar_tensor_tensor(out=acc2[:, b, :], in0=bank[6 + i % 2][:, 0:D], scalar=mean_w[:, b, d:d + 1],
                                             in1=start, op0=ALU.mult, op1=ALU.add).then_inc(ev["half_mean"], 1)
                    dve.wait_ge(ev["half_mean"], gru.four[i])
                    dve.scalar_tensor_tensor(out=acc[:, b, :], in0=bank[6 + i % 2][:, D:2 * D], scalar=mean_w[:, b, d + 1:d + 2],
                                             in1=acc2[:, b, :], op0=ALU.mult, op1=ALU.add).then_inc(ev["mean"], 1)

                if gru:
                    dve.wait_ge(ev["hT_hi"], gru.now)
                    dve.tensor_tensor(hT[1][:, :, :], halves(bank[6][:, :]), as_f32(hT[0][:, :, :]), ALU.subtract).then_inc(ev["hT_lo"], 1)
                each(turned)
                each(keeps, (1, 0))
                if gru:
                    Y_lo(0)
                    Y_lo(1)
                each(projected)
                if gru:
                    dve.wait_ge(ev["mask_m_done"], gru.now)
                    dve.tensor_reduce(count[:, :, :], mask_m[:, :, :, :], AX.X, ALU.add).then_inc(ev["count_done"], 1)
                    dve.wait_ge(ev["count_done"], gru.now)
                    dve.tensor_scalar(count_eps[:, :, :], count[:, :, :], COUNT_EPS, None, ALU.add).then_inc(ev["count_eps_done"], 1)
                    dve.wait_ge(ev["count_eps_done"], gru.now)
                    dve.reciprocal(mean_w[:, :, :], count_eps[:, :, :]).then_inc(ev["mean_w_done"], 1)
                    Y_lo(2)
                    Y_lo(3)
                each(peaks)
                if gru:
                    dve.wait_ge(ev["mean_w_done"], gru.now)
                    wait(dve, ev["oT_psum"], gru.before)
                    for i in range(4):
                        mean(i)
                each(shares)
                each(probs_turned)
                if gru:
                    dve.wait_ge(ev["oT_hi"], gru.now)
                    dve.scalar_tensor_tensor(out=oT[1][:, :, :], in0=halves(bank[6][:, :]), scalar=0.0, in1=as_f32(oT[0][:, :, :]),
                                             op0=ALU.max, op1=ALU.subtract).then_inc(ev["oT_lo"], 1)
                each(attended)
                if gru:
                    dve.wait_ge(ev["nh_psum"], gru.now)
                    dve.wait_ge(ev["r_done"], gru.now)
                    for m in range(C):
                        last = dve.scalar_tensor_tensor(out=hn[:, m, :], in0=bank[6][:, m * TOK:(m + 1) * TOK], scalar=cols[:, 14 + m:15 + m],
                                                        in1=r_gate[:, m, :], op0=ALU.add, op1=ALU.mult)
                    last.then_inc(ev["hn_done"], 1)
                    dve.wait_ge(ev["hn_done"], gru.now)
                    dve.wait_ge(ev["ni_psum"], gru.now)
                    dve.tensor_tensor(pre[:, :, :], halves(bank[6][:, :]), hn[:, :, :], ALU.add).then_inc(ev["pre_done"], 1)
                    dve.wait_ge(ev["n_done"], gru.now)
                    dve.tensor_tensor(diff[:, :, :], hT_full[:, :, :], n_gate[:, :, :], ALU.subtract).then_inc(ev["diff_done"], 1)
                    dve.wait_ge(ev["diff_done"], gru.now)
                    dve.wait_ge(ev["z_done"], gru.now)
                    dve.tensor_tensor(diff[:, :, :], diff[:, :, :], z_gate[:, :, :], ALU.mult).then_inc(ev["zdiff_done"], 1)
                    dve.wait_ge(ev["zdiff_done"], gru.now)
                    wait(dve, ev["new_psum"], gru.before)
                    dve.tensor_tensor(newT[:, :, :], diff[:, :, :], n_gate[:, :, :], ALU.add).then_inc(ev["newT_done"], 1)
                    dve.wait_ge(ev["new_psum"], gru.now)
                    norm(result, halves(bank[7][:, :]), stats3, ev["stats3"], mv3, ev["mv3"], rstd3, ev["rstd3"], ev["z3"],
                         [(ev["stored"], bytes_landed(gru.before))], gru)

            turns(dve, STAGES, groups, step, fourfold=3)

        @block.tensor
        def _(pe):
            pe.wait_ge(load["setup_done"], 3)
            pe.wait_ge(load["graw_landed1"], 16)
            two = raw[:, 1, :].rearrange("p (w c n) -> p w c n", w=4, c=C)
            for k in range(2):
                for m in range(C):
                    for c in range(C):
                        last = pe.matmul(bank[k][:, m * D:(m + 1) * D], two[:, 2 * k, c, m * P:(m + 1) * P], two[:, 2 * k + 1, c, :],
                                         start=c == 0, stop=c == C - 1, skip_group_check=True)
                last.then_inc(load["fused_psum"], 1)
            pe.wait_ge(load["glo_done"], 5)

            def transposes(out, src):
                for c in range(C):
                    for b in range(PAIR):
                        last = pe.transpose(out[:, c * TOK + b * P:c * TOK + (b + 1) * P], src[:, b, c * P:(c + 1) * P], ident[:, :])
                return last

            def product(out, stationary, moving):
                for i, (s, m) in enumerate(zip(stationary, moving)):
                    last = split_product(pe, out, s, m, i == 0, i == len(stationary) - 1)
                return last

            def turned(a, turn):
                if a.n == 0:
                    pe.wait_ge(ev["gx_landed"], bytes_landed(turn.now))
                else:
                    pe.wait_ge(A[a.n - 1]["x_done"], turn.now)
                wait(pe, a["xr_done"], turn.before)
                transposes(bank[a.base], x[a.n]).then_inc(a["xT_psum"], 1)

            def projected(a, turn):
                pe.wait_ge(a["xT_lo"], turn.now)
                if a.n < 2:
                    own = [t[:, a.n, :] for t in w1]
                    for i in range(2):
                        last = product(bank[a.base][:, i * TOK:(i + 1) * TOK],
                                       [[t[:, i * 256 + c * P:i * 256 + (c + 1) * P] for t in own] for c in range(C)],
                                       [[t[:, c, :] for t in a.xT] for c in range(C)])
                    wy = [[t[:, 512 + c * D:512 + (c + 1) * D] for t in own] for c in range(C)]
                else:
                    for m in range(C):
                        last = product(bank[a.base][:, m * TOK:(m + 1) * TOK],
                                       [[t[:, 0, c, m * P:(m + 1) * P] for t in w2] for c in range(C)],
                                       [[t[:, c, :] for t in a.xT] for c in range(C)])
                    wy = [[t[:, 1, c, :] for t in w2] for c in range(C)]
                last.then_inc(a["q_psum"], 1)
                wait(pe, a["probT_lo"], turn.before)
                for b in range(PAIR):
                    last = product(bank[a.base + 1][:, b * D:(b + 1) * D],
                                   [[t[:, c, b * P:(b + 1) * P] for t in a.xT] for c in range(C)], wy)
                last.then_inc(a["y_psum"], 1)

            def scores(a, turn):
                pe.wait_ge(a["q_done"], turn.now)
                for b in range(PAIR):
                    tok = slice(b * P, (b + 1) * P)
                    if a.n < 2:
                        last = pe.matmul(bank[a.base][:, tok], a.q[:, 0, tok], a.q[:, 1, tok], start=True, stop=True, skip_group_check=True)
                    else:
                        for c in range(C):
                            last = pe.matmul(bank[a.base][:, tok], a.q[:, c, tok], a.xT_full[:, c, tok], start=c == 0, stop=c == C - 1, skip_group_check=True)
                last.then_inc(a["scores"], 1)

            def probs_turned(a, turn):
                pe.wait_ge(a["exp"], turn.now)
                pe.wait_ge(a["y_lo"], turn.now)
                for b in range(PAIR):
                    last = pe.transpose(bank[a.base + 1][:, b * P:(b + 1) * P], a.prob[:, b, :], ident[:, :])
                last.then_inc(a["probT_psum"], 1)

            def attend(a, turn):
                pe.wait_ge(a["probT_lo"], turn.now)
                for b in range(PAIR):
                    last = product(bank[a.base][:, b * D:(b + 1) * D], [[t[:, b, :] for t in a.probT]], [[t[:, b, :] for t in a.y]])
                last.then_inc(a["ctx_psum"], 1)

            def step(*stage):
                gru = stage[3]

                def each(f, ns=(2, 1, 0)):
                    for n in ns:
                        if stage[n]:
                            f(A[n], stage[n])

                def labels(i):
                    b, half = i // 2, i % 2
                    if i < 2:
                        pe.wait_ge(ev["hT_lo"], gru.now)
                    if i == 1:
                        wait(pe, ev["z3"], gru.before)
                    if i >= 2:
                        pe.wait_ge(ev["Y_lo"], gru.four[i - 2])
                    product(bank[6 + i % 2][:, :], [[t[:, c, b * P:(b + 1) * P] for t in hT] for c in range(C)],
                            [[t[:, c, half * 512:(half + 1) * 512] for t in wd] for c in range(C)]).then_inc(ev["Y_psum"], 1)

                def aggregate(i):
                    b, half = i // 2, i % 2
                    if i == 0:
                        pe.wait_ge(ev["maskT_done"], gru.now)
                    if i < 2:
                        pe.wait_ge(ev["Y_lo"], gru.four[i + 2])
                    else:
                        pe.wait_ge(ev["mean"], gru.four[i - 2])
                    for k in range(2):
                        d = 2 * half + k
                        for part in (1, 0):
                            last = pe.matmul(bank[6 + i % 2][:, k * D:(k + 1) * D], maskT[:, b, d, :], Y[part][:, b, d * D:(d + 1) * D],
                                             start=part == 1, stop=part == 0, skip_group_check=True)
                    last.then_inc(ev["sums"], 1)

                def gate(out, i_w, h_w, done):
                    for m in range(C):
                        s, mv = [], []
                        for w, act_ in ((i_w, oT), (h_w, hT)):
                            if w is not None:
                                s += [[t[:, w, c, m * P:(m + 1) * P] for t in wg] for c in range(C)]
                                mv += [[t[:, c, :] for t in act_] for c in range(C)]
                        last = product(out[:, m * TOK:(m + 1) * TOK], s, mv)
                    last.then_inc(done, 1)

                if gru:
                    pe.wait_ge(A[2]["x_done"], gru.now)
                    wait(pe, ev["pre_done"], gru.before)
                    transposes(bank[6], x[3]).then_inc(ev["hT_psum"], 1)
                each(turned)
                if gru:
                    labels(0)
                    labels(1)
                each(projected)
                if gru:
                    labels(2)
                    labels(3)
                each(scores)
                if gru:
                    for i in range(4):
                        aggregate(i)
                each(probs_turned)
                if gru:
                    pe.wait_ge(ev["mean"], gru.four[3])
                    transposes(bank[6], acc).then_inc(ev["oT_psum"], 1)
                each(attend)
                if gru:
                    pe.wait_ge(ev["oT_lo"], gru.now)
                    gate(bank[7], 0, 1, ev["r_psum"])
                    gate(bank[6], None, 5, ev["nh_psum"])
                    pe.wait_ge(ev["r_tanh"], gru.now)
                    gate(bank[7], 2, 3, ev["z_psum"])
                    pe.wait_ge(ev["hn_done"], gru.now)
                    gate(bank[6], 4, None, ev["ni_psum"])
                    pe.wait_ge(ev["z_tanh"], gru.now)
                    pe.wait_ge(ev["newT_done"], gru.now)
                    for b in range(PAIR):
                        for c in range(C):
                            last = pe.transpose(bank[7][:, b * D + c * P:b * D + (c + 1) * P], newT[:, c, b * P:(b + 1) * P], ident[:, :])
                    last.then_inc(ev["new_psum"], 1)

            turns(pe, STAGES, groups, step, fourfold=3)


def build(nc, x, adj, adjT, w_a, cols_a, rows_a, w_b, cols_b, rows_b, out):
    x2 = nc.dram_tensor("x2_rows", x.shape, F32, kind="Internal").ap()
    taken = encoder_phase(nc, x, adj, w_a, cols_a, rows_a, x2)
    nc.all_engine_barrier()
    nc.clear_and_free_semaphores(taken)
    nc.all_engine_barrier()
    graph_phase(nc, x2, adj, adjT, w_b, cols_b, rows_b, out)


def kernel(**inputs):
    import numpy as np
    import concourse.bacc as bacc
    from concourse.bass_utils import run_bass_kernel_spmd

    a = {k: np.asarray(v) for k, v in inputs.items()}

    def chunks(w):
        return w.reshape(-1, P, w.shape[1]).transpose(1, 0, 2).reshape(P, -1)

    def col(v):
        return v.reshape(-1, P).T

    L0, L1, L2, L3 = "L0_gnn_", "L1_gnn_", "L2_gnn_", "L3_gnn_"
    w_a = np.concatenate([chunks(a[L0 + n]) for n in ("wq", "wk", "wv", "wo", "w1", "w2")], axis=1)
    cols_a = np.concatenate([col(a[L0 + n]) for n in ("bq", "bk", "b1")], axis=1)
    rows_a = np.stack([a[L0 + n] for n in ("ln1_g", "ln1_b", "bv", "bo", "ln2_g", "ln2_b", "b2")])
    wd = a[L3 + "Wd"].reshape(D, LABELS, D).transpose(2, 1, 0).reshape(D, LABELS * D)
    w_b = np.concatenate(
        [chunks(a[L1 + n][l].T) for l in range(2) for n in ("Wq", "Wk", "Wc")]
        + [chunks(a[L2 + "Wq"].T), chunks(a[L2 + "Wk"].T), chunks(a[L2 + "Wv"].T), chunks(a[L2 + "Wo"]), chunks(wd)]
        + [chunks(a[L3 + n].T) for n in ("Wri", "Wrh", "Wzi", "Wzh", "Wni", "Wnh")], axis=1)
    cols_b = np.concatenate([col(a[L1 + n][l]) for l in range(2) for n in ("bq", "bk")]
                            + [col(a[L3 + n]) for n in ("bri", "brh", "bzi", "bzh", "bni", "bnh")], axis=1)
    rows_b = np.stack([a[L1 + "ln_g"][0], a[L1 + "ln_b"][0], a[L1 + "ln_g"][1], a[L1 + "ln_b"][1], a[L2 + "bo"],
                       a[L2 + "gamma"], a[L2 + "beta"], a[L3 + "bd"], a[L3 + "gamma"], a[L3 + "beta"]])
    laid = {"x": a["x"], "adj": a["adj"], "adjT": a["adj"].transpose(0, 2, 1), "w_a": w_a, "cols_a": cols_a,
            "rows_a": rows_a, "w_b": w_b, "cols_b": cols_b, "rows_b": rows_b}
    laid = {"in_" + k: np.ascontiguousarray(v) for k, v in laid.items()}

    nc = bacc.Bacc("TRN2", target_bir_lowering=False, num_devices=1)
    args = [nc.dram_tensor(k, v.shape, mybir.dt.from_np(v.dtype), kind="ExternalInput").ap() for k, v in laid.items()]
    out = nc.dram_tensor("out_rows", a["x"].shape, F32, kind="ExternalOutput").ap()
    build(nc, *args, out)
    r = run_bass_kernel_spmd(nc, [laid], core_ids=[0])
    return r.results[0]["out_rows"]
```

```python
from contextlib import ExitStack

import concourse.bass as bass
from concourse import mybir

P = 128
D = 256
CH = 2048
HEADS, HD = 8, 32
QUADS = P // HD
C = D // P
PAIR = 2
TOK = PAIR * P
FF = 4 * D
FC = FF // P
LABELS = 4

F32 = mybir.dt.float32
F32R = mybir.dt.float32r
I32 = mybir.dt.int32
ALU = mybir.AluOpType
ACT = mybir.ActivationFunctionType
AX = mybir.AxisListType

MASKED = -1e30
LOWEST = -3.0e38
LN_EPS = 1e-5
COUNT_EPS = 1e-8



def split_product(pe, out, stationary, moving, start, stop):
    s_hi, s_lo = stationary
    m_hi, m_lo = moving
    pe.matmul(out, s_lo, m_hi, start=start, stop=False, skip_group_check=True)
    pe.matmul(out, s_hi, m_lo, start=False, stop=False, skip_group_check=True)
    return pe.matmul(out, s_hi, m_hi, start=False, stop=stop, skip_group_check=True)




def wait(eng, sem, value):
    if value is not None:
        eng.wait_ge(sem, value)


def apart(eng):
    eng.nop(nofuse=True)


class Turn:

    def __init__(self, group, now, before, four=None):
        self.group, self.now, self.before, self.four = group, now, before, four


def pipeline(eng, groups, order, pieces, after=None):
    least = min(lag for _, lag in order)
    order = [(pieces[name], lag - least) for name, lag in order]
    most = max(lag for _, lag in order)

    def peeled(t):
        for piece, lag in order:
            g = t - lag
            if 0 <= g < groups:
                piece(Turn(g, g + 1, g if g > 0 else None, [4 * g + 1 + i for i in range(4)]))

    for t in range(most + 1):
        peeled(t)
        if after and t in after:
            after[t]()
    with eng.Fori(most + 1, groups) as t:
        at = [t if n == 1 else eng.snap(t + (1 - n)) for n in range(most + 2)]
        quads = {}

        def four(lag):
            if lag not in quads:
                quads[lag] = [eng.snap(at[lag + 1] * 4 + (1 + i)) for i in range(4)]
            return quads[lag]

        for piece, lag in order:
            piece(Turn(at[lag + 1], at[lag], at[lag + 1], Four(four, lag)))
    for t in range(groups, groups + most):
        peeled(t)


class Four:

    def __init__(self, four, lag):
        self.four, self.lag = four, lag

    def __getitem__(self, i):
        return self.four(self.lag)[i]


def four_before(turn):
    return None if turn.before is None else turn.before * 4


def bytes_landed(value):
    return None if value is None else value * 16


def declare(ctx, nc):
    def sb(name, shape, dt=F32):
        return ctx.enter_context(nc.sbuf_tensor(name, shape, dt))

    def pair(name, shape):
        return sb(name + "_hi", shape, F32R), sb(name + "_lo", shape, F32R)

    def sems(names):
        got = {n: nc.alloc_semaphore(name=n) for n in names.split()}
        taken.extend(got.values())
        return got

    taken = []
    return sb, pair, sems, taken


def as_f32(ap):
    return ap.bitcast(F32)


ENCODER_ORDER = {
    "pe": [("wo", 4), ("q", 2), ("probs_turned0", 3), ("up1", 5), ("up2", 5), ("probs_turned1", 3), ("scores0", 2), ("up3", 5), ("down0", 5), ("scores1", 2), ("down1", 5), ("attend0", 3), ("nx_turned", 1), ("v", 2), ("n2_turned", 4), ("down2", 5), ("attend1", 3), ("down3", 5), ("k", 1), ("up0", 4)],
    "dve": [("apply1", 1), ("k_lo", 2), ("x1", 4), ("diag_lo", 2), ("probT_lo0", 3), ("q_lo", 2), ("hid_split0", 5), ("hid_split1", 5), ("peaks0", 2), ("apply2", 4), ("probT_lo1", 3), ("peaks1", 2), ("hid_split2", 5), ("hid_split3", 5), ("shares0", 2), ("n2T_lo", 4), ("nxT_lo", 1), ("stats1", 0), ("x2", 5), ("v_full", 2), ("shares1", 2), ("att_split", 3)],
    "act": [("probT_hi1", 2), ("gelu3", 4), ("exps0", 1), ("att_diag0", 2), ("nxT_hi", 0), ("n2T_hi", 3), ("exps1", 1), ("att_diag1", 2), ("k_hi", 0), ("gelu0", 3), ("q_hi", 0), ("probT_hi0", 1), ("gelu1", 3), ("diag_hi", 0), ("gelu2", 3), ("v_hi", 1)],
    "pool": [("x1_plus_b2", 5), ("root1", 1), ("probs1", 3), ("edge_bias", 2), ("affine1", 1), ("root2", 4), ("v_lo", 3), ("affine2", 4), ("x_plus_bo", 3), ("probs0", 2)],
    "sp": [("load_x_again", 3), ("load_x", 0), ("store_x2", 5), ("load_adj", 0)],
}


def encoder_phase(nc, x, adj, w_dram, cols_dram, rows_dram, x2_dram, raw, next_w_dram):
    groups = x.shape[0] // PAIR
    x_g = x.rearrange("(g b) p d -> g p b d", b=PAIR)
    adj_g = adj.rearrange("(g b) p k -> g p b k", b=PAIR)
    x2_g = x2_dram.rearrange("(g b) p d -> g p b d", b=PAIR)
    scale = float(HD) ** -0.5
    bias_scale = 0.1 * float(HD) ** 0.5
    n_w = w_dram.shape[1] // CH

    with ExitStack() as ctx:
        sb, pair, sems, taken = declare(ctx, nc)
        att_w = pair("att_w", [P, 4, C, D])
        w1 = pair("w1", [P, C, FF])
        w2 = pair("w2", [P, FC, D])
        flat = [[t[:, :].rearrange("p a c n -> p (a c n)") if len(t.shape) == 4 else
                 t[:, :].rearrange("p a n -> p (a n)") for t in w] for w in (att_w, w1, w2)]
        cols = sb("cols", [P, 2 * C + FC])
        rows = sb("rows", [P, 7, D])
        LN1_G, LN1_B, BV, BO, LN2_G, LN2_B, B2 = range(7)
        ident = sb("ident", [P, P])
        power = sb("power", [P, PAIR])

        x_in = sb("x_in", [P, PAIR, D])
        adj_in = sb("adj_in", [P, PAIR, P], I32)
        stats1 = sb("stats1", [P, PAIR, 6])
        mv1 = sb("mv1", [P, PAIR, 2])
        var1 = sb("var1", [P, PAIR])
        rstd1 = sb("rstd1", [P, PAIR])
        nx = sb("nx", [P, PAIR, D])
        masked = sb("masked", [P, PAIR, P])
        adj_f = sb("adj_f", [P, PAIR, P])
        scaled = sb("scaled", [P, PAIR, P])
        squares = sb("squares", [P, PAIR, P])
        edge_bias = sb("edge_bias", [P, PAIR, P])
        nxT = pair("nxT", [P, C, TOK])
        qT = pair("qT", [P, C, TOK])
        kT = pair("kT", [P, C, TOK])
        k_diag = pair("k_diag", [P, PAIR, C, QUADS, P])
        v_full = sb("v_full", [P, PAIR, D])
        v = pair("v", [P, PAIR, D])
        prob = sb("prob", [P, PAIR, HEADS, P])
        peak = sb("peak", [P, PAIR, HEADS])
        shift = sb("shift", [P, PAIR, HEADS])
        total = sb("total", [P, PAIR, HEADS])
        share = sb("share", [P, PAIR, HEADS])
        probT = pair("probT", [P, PAIR, C, QUADS, P])
        att_full = sb("att_full", [P, C, TOK])
        attT = pair("attT", [P, C, TOK])
        x_again = sb("x_again", [P, PAIR, D])
        x_bo = sb("x_bo", [P, PAIR, D])
        x1 = sb("x1", [P, PAIR, D])
        x1_b2 = sb("x1_b2", [P, PAIR, D])
        stats2 = sb("stats2", [P, PAIR, 6])
        mv2 = sb("mv2", [P, PAIR, 2])
        var2 = sb("var2", [P, PAIR])
        rstd2 = sb("rstd2", [P, PAIR])
        n2 = sb("n2", [P, PAIR, D])
        n2T = pair("n2T", [P, C, TOK])
        hid_full = [sb(f"hid_full{i}", [P, 2, TOK]) for i in range(2)]
        hidT = [pair(f"hidT{i}", [P, 2, TOK]) for i in range(2)]
        x2 = sb("x2", [P, PAIR, D])

        bank = [ctx.enter_context(nc.psum_tensor(f"bank{i}", [P, 512], F32)) for i in range(8)]

        load = sems("raw_landed0 raw_landed1 next_landed hi_done lo_done const_landed zeroed ident_zero ident_done")
        ev = sems(
            "x_landed adj_landed x_again_landed x2_stored "
            "stats1_done mv1_done var1_done rstd1_done z1_done g1_done nx_done "
            "masked_done squares_done scaled_done edge_bias_done "
            "nxT_psum nxT_hi nxT_lo q_psum k_psum v_psum q_hi k_hi q_lo k_lo diag_hi diag_lo "
            "v_full_done v_hi v_lo "
            "scores0 scores1 peak0 peak1 shift0 shift1 exp0 exp1 share0 share1 prob0 prob1 "
            "probT_psum0 probT_psum1 probT_hi0 probT_hi1 probT_lo0 probT_lo1 att_psum0 att_psum1 "
            "att_full0 att_full1 att_hi att_lo wo_psum x_bo_done x1_done x1_b2_done "
            "stats2_done mv2_done var2_done rstd2_done z2_done g2_done n2_done "
            "n2T_psum n2T_hi n2T_lo up0 up1 up2 up3 gelu0 gelu1 gelu2 gelu3 "
            "hid_hi0 hid_hi1 hid_hi2 hid_hi3 hid_lo0 hid_lo1 hid_lo2 hid_lo3 down0 down1 down2 down3 "
            "x2_done")
        block = ctx.enter_context(nc.Block())

        def b_(name, b):
            return ev[f"{name}{b}"]

        def halves(psum):
            return psum[:, :].rearrange("p (c t) -> p c t", c=2)

        def heads_of(psum):
            return psum[:, :].rearrange("p (h k) -> p h k", h=QUADS)

        QK_BANK = {"q": bank[1], "k": bank[2]}

        @block.sync
        def _(sp):
            sp.dma_start(cols[:, :], cols_dram).then_inc(load["const_landed"], 16)
            sp.dma_start(rows[:, :, :], rows_dram.partition_broadcast(P)).then_inc(load["const_landed"], 16)
            for n in range(n_w):
                if n >= 2:
                    sp.wait_ge(load["lo_done"], n - 1)
                sp.dma_start(raw[:, n % 2, :], w_dram[:, n * CH:(n + 1) * CH]).then_inc(load[f"raw_landed{n % 2}"], 16)

            def load_x(g):
                wait(sp, ev["z1_done"], g.before)
                sp.dma_start(x_in[:, :, :], x_g[g.group]).then_inc(ev["x_landed"], 16)

            def load_adj(g):
                wait(sp, ev["scaled_done"], g.before)
                sp.dma_start(adj_in[:, :, :], adj_g[g.group]).then_inc(ev["adj_landed"], 16)

            def load_x_again(g):
                wait(sp, ev["x_bo_done"], g.before)
                sp.dma_start(x_again[:, :, :], x_g[g.group]).then_inc(ev["x_again_landed"], 16)

            def store_x2(g):
                sp.wait_ge(ev["x2_done"], g.now)
                sp.dma_start(x2_g[g.group], x2[:, :, :]).then_inc(ev["x2_stored"], 16)

            def load_next_weights():
                sp.wait_ge(load["lo_done"], n_w)
                sp.dma_start(raw[:, :, :].rearrange("p a n -> p (a n)"), next_w_dram[:, 0:2 * CH]).then_inc(load["next_landed"], 16)

            pipeline(sp, groups, ENCODER_ORDER["sp"], dict(
                load_x=load_x, load_adj=load_adj, load_x_again=load_x_again, store_x2=store_x2),
                after={3: load_next_weights})
            sp.wait_ge(load["next_landed"], 16)
            sp.wait_ge(ev["x2_stored"], 16 * groups)

        @block.gpsimd
        def _(pool):
            pool.memset(power[:, :], -0.5).then_inc(load["ident_zero"], 1)
            pool.memset(ident[:, :], 0.0).then_inc(load["ident_zero"], 1)
            pool.wait_ge(load["ident_zero"], 2)
            pool.affine_select(out=ident[:, :], in_=ident[:, :], compare_op=ALU.not_equal, fill=1.0, base=0,
                               pattern=[[-1, P]], channel_multiplier=1).then_inc(load["ident_done"], 1)
            pool.wait_ge(load["const_landed"], 32)

            def row(i):
                return rows[:, i:i + 1, :].broadcast_to([P, PAIR, D])

            def reciprocal_root(mv_done, mv, var, var_done, rstd, rstd_done, turn):
                pool.wait_ge(mv_done, turn.now)
                apart(pool)
                pool.tensor_scalar(var[:, :], mv[:, :, 1], LN_EPS, None, ALU.add).then_inc(var_done, 1)
                pool.wait_ge(var_done, turn.now)
                pool.tensor_tensor(rstd[:, :], var[:, :], power[:, :], ALU.pow).then_inc(rstd_done, 1)

            def edge_bias_(g):
                pool.wait_ge(ev["adj_landed"], bytes_landed(g.now))
                apart(pool)
                pool.tensor_scalar(masked[:, :, :], adj_in[:, :, :], 0.0, MASKED, ALU.is_le, ALU.mult).then_inc(ev["masked_done"], 1)
                pool.tensor_scalar(adj_f[:, :, :], adj_in[:, :, :], 1.0, None, ALU.mult)
                pool.tensor_scalar(scaled[:, :, :], adj_in[:, :, :], bias_scale, None, ALU.mult).then_inc(ev["scaled_done"], 1)
                pool.wait_ge(ev["scaled_done"], g.now)
                pool.tensor_tensor(squares[:, :, :], scaled[:, :, :], adj_f[:, :, :], ALU.mult).then_inc(ev["squares_done"], 1)
                pool.wait_ge(ev["squares_done"], g.now)
                pool.tensor_tensor(edge_bias[:, :, :], squares[:, :, :], masked[:, :, :], ALU.add).then_inc(ev["edge_bias_done"], 1)

            def x_plus_bo(g):
                pool.wait_ge(ev["x_again_landed"], bytes_landed(g.now))
                pool.tensor_tensor(x_bo[:, :, :], x_again[:, :, :], row(BO), ALU.add).then_inc(ev["x_bo_done"], 1)

            def probs(b):
                def piece(g):
                    pool.wait_ge(b_("share", b), g.now)
                    pool.tensor_tensor(prob[:, b, :, :], prob[:, b, :, :],
                                       share[:, b, :].unsqueeze(2).broadcast_to([P, HEADS, P]),
                                       ALU.mult).then_inc(b_("prob", b), 1)
                return piece

            def root1(g):
                reciprocal_root(ev["mv1_done"], mv1, var1, ev["var1_done"], rstd1, ev["rstd1_done"], g)

            def affine1(g):
                pool.wait_ge(ev["z1_done"], g.now)
                pool.tensor_tensor(nx[:, :, :], nx[:, :, :], row(LN1_G), ALU.mult).then_inc(ev["g1_done"], 1)
                pool.wait_ge(ev["g1_done"], g.now)
                pool.tensor_tensor(nx[:, :, :], nx[:, :, :], row(LN1_B), ALU.add).then_inc(ev["nx_done"], 1)

            def root2(g):
                reciprocal_root(ev["mv2_done"], mv2, var2, ev["var2_done"], rstd2, ev["rstd2_done"], g)

            def affine2(g):
                pool.wait_ge(ev["z2_done"], g.now)
                pool.tensor_tensor(n2[:, :, :], n2[:, :, :], row(LN2_G), ALU.mult).then_inc(ev["g2_done"], 1)
                pool.wait_ge(ev["g2_done"], g.now)
                pool.tensor_tensor(n2[:, :, :], n2[:, :, :], row(LN2_B), ALU.add).then_inc(ev["n2_done"], 1)

            def x1_plus_b2(g):
                wait(pool, ev["x2_done"], g.before)
                pool.tensor_tensor(x1_b2[:, :, :], x1[:, :, :], row(B2), ALU.add).then_inc(ev["x1_b2_done"], 1)

            def v_lo(g):
                pool.wait_ge(ev["v_hi"], g.now)
                pool.tensor_tensor(v[1][:, :, :], v_full[:, :, :], as_f32(v[0][:, :, :]), ALU.subtract).then_inc(ev["v_lo"], 1)

            pipeline(pool, groups, ENCODER_ORDER["pool"], dict(
                edge_bias=edge_bias_, x_plus_bo=x_plus_bo, probs0=probs(0), probs1=probs(1), root1=root1, affine1=affine1,
                root2=root2, affine2=affine2, x1_plus_b2=x1_plus_b2, v_lo=v_lo))

        @block.scalar
        def _(act):
            for n in range(n_w):
                act.wait_ge(load[f"raw_landed{n % 2}"], 16 * (n // 2 + 1))
                act.activation(flat[n][0], raw[:, n % 2, :], ACT.Copy).then_inc(load["hi_done"], 1)
            act.wait_ge(load["const_landed"], 32)

            def probT_hi(b):
                def piece(g):
                    act.wait_ge(b_("probT_psum", b), g.now)
                    for c in range(C):
                        last = act.activation(probT[0][:, b, c, :, :], heads_of(bank[4 + c]), ACT.Copy)
                    last.then_inc(b_("probT_hi", b), 1)
                return piece

            def att_diag(b):
                def piece(g):
                    act.wait_ge(b_("att_psum", b), g.now)
                    for c in range(C):
                        for j in range(QUADS):
                            own = slice(HD * j, HD * (j + 1))
                            last = act.activation(att_full[own, c, b * P:(b + 1) * P], bank[4 + c][own, j * P:(j + 1) * P], ACT.Copy)
                    last.then_inc(b_("att_full", b), 1)
                return piece

            def exps(b):
                def piece(g):
                    act.wait_ge(b_("shift", b), g.now)
                    for h in range(HEADS):
                        last = act.activation(prob[:, b, h, :], prob[:, b, h, :], ACT.Exp, bias=shift[:, b, h:h + 1],
                                              scale=scale, accum_out=total[:, b, h:h + 1])
                    last.then_inc(b_("exp", b), 1)
                return piece

            def gelu(p):
                def piece(g):
                    act.wait_ge(b_("up", p), g.now)
                    if p >= 2:
                        act.wait_ge(b_("hid_lo", p - 2), g.now)
                    for j in range(2):
                        f = 2 * C + 2 * p + j
                        last = act.activation(hid_full[p % 2][:, j, :], bank[6][:, j * TOK:(j + 1) * TOK], ACT.Gelu, bias=cols[:, f:f + 1])
                    last.then_inc(b_("gelu", p), 1)
                return piece

            def n2T_hi(g):
                act.wait_ge(ev["n2T_psum"], g.now)
                act.activation(n2T[0][:, :, :], halves(bank[6]), ACT.Copy).then_inc(ev["n2T_hi"], 1)

            def nxT_hi(g):
                act.wait_ge(ev["nxT_psum"], g.now)
                wait(act, ev["v_psum"], g.before)
                act.activation(nxT[0][:, :, :], halves(bank[0]), ACT.Copy).then_inc(ev["nxT_hi"], 1)

            def biased_hi(name, dst, bias_at):
                def piece(g):
                    act.wait_ge(ev[name + "_psum"], g.now)
                    for m in range(C):
                        last = act.activation(dst[0][:, m, :], QK_BANK[name][:, m * TOK:(m + 1) * TOK], ACT.Identity,
                                              bias=cols[:, bias_at + m:bias_at + m + 1])
                    last.then_inc(ev[name + "_hi"], 1)
                return piece

            def diag_hi(g):
                act.wait_ge(ev["k_hi"], g.now)
                for j in range(QUADS):
                    own = slice(HD * j, HD * (j + 1))
                    last = act.activation(k_diag[0][own, :, :, j, :],
                                          as_f32(kT[0][own, :, :]).rearrange("p c (b k) -> p b c k", b=PAIR), ACT.Copy)
                last.then_inc(ev["diag_hi"], 1)

            def v_hi(g):
                act.wait_ge(ev["v_full_done"], g.now)
                act.activation(v[0][:, :, :], v_full[:, :, :], ACT.Copy).then_inc(ev["v_hi"], 1)

            pipeline(act, groups, ENCODER_ORDER["act"], dict(
                nxT_hi=nxT_hi, q_hi=biased_hi("q", qT, 0), k_hi=biased_hi("k", kT, C), diag_hi=diag_hi,
                v_hi=v_hi, exps0=exps(0), exps1=exps(1), probT_hi0=probT_hi(0), probT_hi1=probT_hi(1), att_diag0=att_diag(0),
                att_diag1=att_diag(1), n2T_hi=n2T_hi, gelu0=gelu(0), gelu1=gelu(1), gelu2=gelu(2), gelu3=gelu(3)))

        @block.vector
        def _(dve):
            for t in k_diag:
                last = dve.memset(as_f32(t[:, :, :, :, :]), 0.0)
            last.then_inc(load["zeroed"], 1)
            for n in range(n_w):
                dve.wait_ge(load["hi_done"], n + 1)
                dve.tensor_tensor(flat[n][1], raw[:, n % 2, :], as_f32(flat[n][0]), ALU.subtract).then_inc(load["lo_done"], 1)
            dve.wait_ge(load["const_landed"], 32)
            dve.wait_ge(load["zeroed"], 1)

            def norm_stats(src, stats, stats_done, mv, mv_done, g):
                for b in range(PAIR):
                    last = dve.bn_stats(stats[:, b, :], src[:, b, :])
                last.then_inc(stats_done, 1)
                dve.wait_ge(stats_done, g.now)
                apart(dve)
                for b in range(PAIR):
                    last = dve.bn_aggr(mv[:, b, :], stats[:, b, :])
                last.then_inc(mv_done, 1)

            def norm_apply(dst, src, mv, rstd, rstd_done, z_done, g):
                dve.wait_ge(rstd_done, g.now)
                for b in range(PAIR):
                    last = dve.tensor_scalar(dst[:, b, :], src[:, b, :], mv[:, b, 0:1], rstd[:, b:b + 1], ALU.subtract, ALU.mult)
                last.then_inc(z_done, 1)

            def stats1_(g):
                dve.wait_ge(ev["x_landed"], bytes_landed(g.now))
                norm_stats(x_in, stats1, ev["stats1_done"], mv1, ev["mv1_done"], g)

            def apply1(g):
                norm_apply(nx, x_in, mv1, rstd1, ev["rstd1_done"], ev["z1_done"], g)

            def nxT_lo(g):
                dve.wait_ge(ev["nxT_hi"], g.now)
                dve.tensor_tensor(nxT[1][:, :, :], halves(bank[0]), as_f32(nxT[0][:, :, :]), ALU.subtract).then_inc(ev["nxT_lo"], 1)

            def n2T_lo(g):
                dve.wait_ge(ev["n2T_hi"], g.now)
                dve.tensor_tensor(n2T[1][:, :, :], halves(bank[6]), as_f32(n2T[0][:, :, :]), ALU.subtract).then_inc(ev["n2T_lo"], 1)

            def biased_lo(name, dst, bias_at):
                def piece(g):
                    dve.wait_ge(ev[name + "_hi"], g.now)
                    for m in range(C):
                        last = dve.scalar_tensor_tensor(out=dst[1][:, m, :], in0=QK_BANK[name][:, m * TOK:(m + 1) * TOK],
                                                        scalar=cols[:, bias_at + m:bias_at + m + 1], in1=as_f32(dst[0][:, m, :]),
                                                        op0=ALU.add, op1=ALU.subtract)
                    last.then_inc(ev[name + "_lo"], 1)
                return piece

            def diag_lo(g):
                dve.wait_ge(ev["k_lo"], g.now)
                for j in range(QUADS):
                    own = slice(HD * j, HD * (j + 1))
                    last = dve.tensor_copy(k_diag[1][own, :, :, j, :],
                                           as_f32(kT[1][own, :, :]).rearrange("p c (b k) -> p b c k", b=PAIR))
                last.then_inc(ev["diag_lo"], 1)

            def v_full_(g):
                dve.tensor_tensor(v_full[:, :, :], halves(bank[3]), rows[:, BV:BV + 1, :].broadcast_to([P, PAIR, D]),
                                  ALU.add).then_inc(ev["v_full_done"], 1)

            def peaks(b):
                def piece(g):
                    dve.wait_ge(b_("scores", b), g.now)
                    dve.wait_ge(ev["edge_bias_done"], g.now)
                    apart(dve)
                    for h in range(HEADS):
                        last = dve.tensor_tensor_reduce(prob[:, b, h, :], bank[2 * b + h // QUADS][:, (h % QUADS) * P:(h % QUADS + 1) * P],
                                                        edge_bias[:, b, :], 1.0, LOWEST, ALU.add, ALU.max, peak[:, b, h:h + 1])
                    last.then_inc(b_("peak", b), 1)
                    dve.wait_ge(b_("peak", b), g.now)
                    dve.tensor_scalar(shift[:, b, :], peak[:, b, :], -scale, None, ALU.mult).then_inc(b_("shift", b), 1)
                return piece

            def shares(b):
                def piece(g):
                    dve.wait_ge(b_("exp", b), g.now)
                    dve.reciprocal(share[:, b, :], total[:, b, :]).then_inc(b_("share", b), 1)
                return piece

            def probT_lo(b):
                def piece(g):
                    dve.wait_ge(b_("probT_hi", b), g.now)
                    for c in range(C):
                        last = dve.tensor_tensor(probT[1][:, b, c, :, :], heads_of(bank[4 + c]), as_f32(probT[0][:, b, c, :, :]), ALU.subtract)
                    last.then_inc(b_("probT_lo", b), 1)
                return piece

            def att_split(g):
                dve.wait_ge(ev["att_full1"], g.now)
                dve.wait_ge(ev["att_full0"], g.now)
                dve.tensor_copy(attT[0][:, :, :], att_full[:, :, :]).then_inc(ev["att_hi"], 1)
                dve.wait_ge(ev["att_hi"], g.now)
                dve.tensor_tensor(attT[1][:, :, :], att_full[:, :, :], as_f32(attT[0][:, :, :]), ALU.subtract).then_inc(ev["att_lo"], 1)

            def x1_(g):
                dve.wait_ge(ev["wo_psum"], g.now)
                wait(dve, ev["x1_b2_done"], g.before)
                dve.tensor_tensor(x1[:, :, :], halves(bank[4]), x_bo[:, :, :], ALU.add).then_inc(ev["x1_done"], 1)
                dve.wait_ge(ev["x1_done"], g.now)
                norm_stats(x1, stats2, ev["stats2_done"], mv2, ev["mv2_done"], g)

            def apply2(g):
                norm_apply(n2, x1, mv2, rstd2, ev["rstd2_done"], ev["z2_done"], g)

            def hid_split(p):
                def piece(g):
                    hi, lo = hidT[p % 2]
                    dve.wait_ge(b_("gelu", p), g.now)
                    if p >= 2:
                        dve.wait_ge(b_("down", p - 2), g.now)
                    dve.tensor_copy(hi[:, :, :], hid_full[p % 2][:, :, :]).then_inc(b_("hid_hi", p), 1)
                    dve.wait_ge(b_("hid_hi", p), g.now)
                    dve.tensor_tensor(lo[:, :, :], hid_full[p % 2][:, :, :], as_f32(hi[:, :, :]), ALU.subtract).then_inc(b_("hid_lo", p), 1)
                return piece

            def x2_(g):
                dve.wait_ge(ev["down3"], g.now)
                dve.wait_ge(ev["x1_b2_done"], g.now)
                wait(dve, ev["x2_stored"], bytes_landed(g.before))
                dve.tensor_tensor(x2[:, :, :], halves(bank[7]), x1_b2[:, :, :], ALU.add).then_inc(ev["x2_done"], 1)

            pipeline(dve, groups, ENCODER_ORDER["dve"], dict(
                stats1=stats1_, apply1=apply1, nxT_lo=nxT_lo, q_lo=biased_lo("q", qT, 0), k_lo=biased_lo("k", kT, C), diag_lo=diag_lo,
                v_full=v_full_, peaks0=peaks(0), peaks1=peaks(1), shares0=shares(0), shares1=shares(1), probT_lo0=probT_lo(0),
                probT_lo1=probT_lo(1), att_split=att_split, x1=x1_, apply2=apply2, n2T_lo=n2T_lo, hid_split0=hid_split(0),
                hid_split1=hid_split(1), hid_split2=hid_split(2), hid_split3=hid_split(3), x2=x2_))

        @block.tensor
        def _(pe):
            pe.wait_ge(load["ident_done"], 1)
            pe.wait_ge(load["lo_done"], n_w)

            def transposes(out, src):
                for c in range(C):
                    for b in range(PAIR):
                        last = pe.transpose(out[:, c * TOK + b * P:c * TOK + (b + 1) * P], src[:, b, c * P:(c + 1) * P], ident[:, :])
                return last

            def feature_rows(out, w, which, actT):
                for m in range(C):
                    for c in range(C):
                        last = split_product(pe, out[:, m * TOK:(m + 1) * TOK], [t[:, which, c, m * P:(m + 1) * P] for t in w],
                                             [t[:, c, :] for t in actT], c == 0, c == C - 1)
                return last

            def token_rows(out, w, which, actT):
                for b in range(PAIR):
                    for c in range(C):
                        last = split_product(pe, out[:, b * D:(b + 1) * D], [t[:, c, b * P:(b + 1) * P] for t in actT],
                                             [t[:, which, c, :] for t in w], c == 0, c == C - 1)
                return last

            def nx_turned(g):
                pe.wait_ge(ev["nx_done"], g.now)
                wait(pe, ev["peak0"], g.before)
                transposes(bank[0], nx).then_inc(ev["nxT_psum"], 1)

            def q(g):
                feature_rows(bank[1], att_w, 0, nxT).then_inc(ev["q_psum"], 1)

            def k(g):
                pe.wait_ge(ev["nxT_lo"], g.now)
                feature_rows(bank[2], att_w, 1, nxT).then_inc(ev["k_psum"], 1)

            def v_(g):
                pe.wait_ge(ev["peak1"], g.now)
                token_rows(bank[3], att_w, 2, nxT).then_inc(ev["v_psum"], 1)

            def scores(b):
                def piece(g):
                    if b == 0:
                        pe.wait_ge(ev["q_lo"], g.now)
                        pe.wait_ge(ev["diag_hi"], g.now)
                    for c in range(C):
                        last = split_product(pe, bank[2 * b + c][:, :], [t[:, c, b * P:(b + 1) * P] for t in qT],
                                             [t[:, b, c, :, :].rearrange("p h k -> p (h k)") for t in k_diag], True, True)
                    last.then_inc(b_("scores", b), 1)
                return piece

            def probs_turned(b):
                def piece(g):
                    pe.wait_ge(b_("prob", b), g.now)
                    if b == 0:
                        wait(pe, ev["x1_done"], g.before)
                    else:
                        pe.wait_ge(ev["probT_lo0"], g.now)
                    for h in range(HEADS):
                        last = pe.transpose(bank[4 + h // QUADS][:, (h % QUADS) * P:(h % QUADS + 1) * P], prob[:, b, h, :], ident[:, :])
                    last.then_inc(b_("probT_psum", b), 1)
                return piece

            def attend(b):
                def piece(g):
                    if b == 0:
                        pe.wait_ge(ev["probT_lo1"], g.now)
                        pe.wait_ge(ev["v_lo"], g.now)
                    else:
                        pe.wait_ge(ev["att_full0"], g.now)
                    for c in range(C):
                        last = split_product(pe, bank[4 + c][:, :], [t[:, b, c * P:(c + 1) * P] for t in v],
                                             [t[:, b, c, :, :].rearrange("p h k -> p (h k)") for t in probT], True, True)
                    last.then_inc(b_("att_psum", b), 1)
                return piece

            def wo(g):
                pe.wait_ge(ev["att_lo"], g.now)
                token_rows(bank[4], att_w, 3, attT).then_inc(ev["wo_psum"], 1)

            def n2_turned(g):
                pe.wait_ge(ev["n2_done"], g.now)
                wait(pe, ev["gelu3"], g.before)
                transposes(bank[6], n2).then_inc(ev["n2T_psum"], 1)

            def up(p):
                def piece(g):
                    if p == 0:
                        pe.wait_ge(ev["n2T_lo"], g.now)
                    else:
                        pe.wait_ge(b_("gelu", p - 1), g.now)
                    for j in range(2):
                        f = (2 * p + j) * P
                        for c in range(C):
                            last = split_product(pe, bank[6][:, j * TOK:(j + 1) * TOK], [t[:, c, f:f + P] for t in w1],
                                                 [t[:, c, :] for t in n2T], c == 0, c == C - 1)
                    last.then_inc(b_("up", p), 1)
                return piece

            def down(p):
                def piece(g):
                    pe.wait_ge(b_("hid_lo", p), g.now)
                    for j in range(2):
                        for b in range(PAIR):
                            last = split_product(pe, bank[7][:, b * D:(b + 1) * D], [t[:, j, b * P:(b + 1) * P] for t in hidT[p % 2]],
                                                 [t[:, 2 * p + j, :] for t in w2], p == 0 and j == 0 and b == 0, p == 3 and j == 1)
                    last.then_inc(b_("down", p), 1)
                return piece

            pipeline(pe, groups, ENCODER_ORDER["pe"], dict(
                nx_turned=nx_turned, q=q, k=k, v=v_, scores0=scores(0), scores1=scores(1), probs_turned0=probs_turned(0),
                probs_turned1=probs_turned(1), attend0=attend(0), attend1=attend(1), wo=wo, n2_turned=n2_turned, up0=up(0), up1=up(1),
                up2=up(2), up3=up(3), down0=down(0), down1=down(1), down2=down(2), down3=down(3)))
    return taken


GRAPH_ORDER = {
    "pe": [("probs_turned_1", 2), ("nh", 4), ("attend_1", 2), ("z", 4), ("ni", 4), ("turned_0", 0), ("hid_turned", 3), ("q_0", 0), ("y_0", 0), ("new_turned", 4), ("labels0", 3), ("labels1", 3), ("scores_0", 0), ("turned_2", 2), ("labels2", 3), ("turned_1", 1), ("labels3", 3), ("q_2", 2), ("sums0", 3), ("sums1", 3), ("y_2", 2), ("scores_2", 2), ("sums2", 3), ("q_1", 1), ("sums3", 3), ("probs_turned_0", 0), ("y_1", 1), ("probs_turned_2", 2), ("out_turned", 3), ("scores_1", 1), ("attend_0", 0), ("attend_2", 2), ("r", 3)],
    "dve": [("probT_lo_1", 3), ("residual_0", 2), ("offset_2", 4), ("shares_1", 3), ("gated_nh", 5), ("offset_0", 2), ("residual_1", 3), ("n_before_tanh", 5), ("xT_lo_0", 1), ("offset_1", 3), ("blend", 5), ("hT_lo", 4), ("counts", 4), ("stats_3", 5), ("Y_lo0", 4), ("Y_lo1", 4), ("offset_3", 5), ("xT_lo_2", 3), ("peaks_0", 1), ("xT_lo_1", 2), ("Y_lo2", 4), ("Y_lo3", 4), ("y_lo_0", 1), ("mean0", 4), ("mean1", 4), ("peaks_2", 3), ("mean2", 4), ("y_lo_2", 3), ("mean3", 4), ("shares_2", 3), ("shares_0", 1), ("probT_lo_0", 1), ("probT_lo_2", 3), ("oT_lo", 4), ("peaks_1", 2), ("y_lo_1", 2), ("residual_2", 3)],
    "act": [("q_1", 2), ("probT_hi_0", 1), ("probT_hi_2", 3), ("oT_hi", 4), ("y_hi_1", 2), ("exps_1", 2), ("probT_hi_1", 2), ("r_tanh", 4), ("apply_2", 3), ("z_tanh", 4), ("apply_0", 1), ("xT_hi_0", 0), ("n_tanh", 4), ("hT_hi", 3), ("apply_1", 2), ("new_rows", 4), ("q_0", 0), ("Y_hi0", 3), ("Y_hi1", 3), ("xT_hi_2", 2), ("Y_hi2", 3), ("xT_hi_1", 1), ("y_hi_0", 0), ("Y_hi3", 3), ("exps_0", 0), ("q_2", 2), ("y_hi_2", 2), ("apply_3", 4), ("exps_2", 2)],
    "pool": [("affine_2", 3), ("root_1", 2), ("z_sigmoid", 4), ("affine_0", 1), ("affine_1", 2), ("root_3", 4), ("mask_0", 0), ("mask_2", 2), ("mask_m", 2), ("maskT", 2), ("x_plus_bo", 2), ("affine_3", 4), ("root_2", 2), ("mask_1", 0), ("r_sigmoid", 3), ("root_0", 0)],
    "sp": [("load_x2", 0), ("load_adj_1", 0), ("load_adj_0", 0), ("load_labels", 2), ("load_adj_2", 2), ("store", 4)],
}


def graph_phase(nc, x2_dram, adj, adjT, w_dram, cols_dram, rows_dram, out_dram, raw):
    groups = x2_dram.shape[0] // PAIR
    x2_g = x2_dram.rearrange("(g b) p d -> g p b d", b=PAIR)
    adj_g = adj.rearrange("(g b) p k -> g p b k", b=PAIR)
    adjT_g = adjT.rearrange("(g b) k p -> g k b p", b=PAIR)
    out_g = out_dram.rearrange("(g b) p d -> g p b d", b=PAIR)
    W1, W2, WD, WG = 0, 1024 * 2, 2048 * 2, 2048 * 3
    score_scale = [float(P) ** -0.5, float(P) ** -0.5, float(D) ** -0.5]

    with ExitStack() as ctx:
        sb, pair, sems, taken = declare(ctx, nc)
        w1 = pair("w1_", [P, 2, 1024])
        w2 = pair("w2_", [P, 2, C, D])
        wd = pair("wd", [P, C, LABELS * D])
        wg = pair("wg", [P, 6, C, D])
        cols = sb("cols_", [P, 4 + 12])
        gate_b = sb("gate_b", [P, 2, C])
        gate_sum = sb("gate_sum", [P, 2, C])
        rows = sb("rows_", [P, 10, D])
        NORM_G, NORM_B, BO, BD = [0, 2, 5, 8], [1, 3, 6, 9], 4, 7
        ident = sb("ident_", [P, P])
        power = sb("power_", [P, PAIR])

        class Attention:

            def __init__(self, n):
                def own(name, shape, dt=F32):
                    return sb(f"{name}_{n}", shape, dt)
                self.n = n
                self.adj = own("adj", [P, PAIR, P], I32)
                self.mask = own("mask", [P, PAIR, P])
                self.xT = pair(f"xT_{n}", [P, C, TOK])
                self.xT_full = own("xT_full", [P, C, TOK]) if n == 2 else None
                self.q = own("q", [P, C, TOK])
                self.y = pair(f"y_{n}", [P, PAIR, D])
                self.prob = own("prob", [P, PAIR, P])
                self.peak = own("peak", [P, PAIR])
                self.shift = own("shift", [P, PAIR])
                self.total = own("total", [P, PAIR])
                self.inv = own("inv", [P, PAIR])
                self.share = own("share", [P, PAIR]) if n < 2 else self.inv
                self.probT = pair(f"probT_{n}", [P, PAIR, P])
                self.xr = own("xr", [P, PAIR, D])
                self.stats = own("stats", [P, PAIR, 6])
                self.mv = own("mv", [P, PAIR, 2])
                self.var = own("var", [P, PAIR])
                self.rstd = own("rstd", [P, PAIR])
                self.offset = own("offset", [P, PAIR])
                self.ev = sems(" ".join(f"{e}_{n}" for e in self.EVENTS.split()
                                        if n < 2 or e != "share"))
                self.base = 2 * n

            EVENTS = ("adj_landed mask_done xT_psum xT_hi xT_lo q_psum y_psum q_done y_hi y_lo "
                      "scores peak shift exp inv share probT_psum probT_hi probT_lo ctx_psum xr_done stats mv var rstd "
                      "offset z g x_done")

            def __getitem__(self, name):
                if name == "share" and self.n == 2:
                    name = "inv"
                return self.ev[f"{name}_{self.n}"]

        x_in = sb("x_in_", [P, PAIR, D])
        x = [x_in] + [sb(f"x_{n}", [P, PAIR, D]) for n in range(1, 4)]
        A = [Attention(n) for n in range(3)]
        x_bo = sb("x_bo_", [P, PAIR, D])

        adjT_in = sb("adjT_in", [P, PAIR, P], I32)
        adj_in = sb("adj_in_", [P, PAIR, P], I32)
        maskT = sb("maskT", [P, PAIR, LABELS, P], F32R)
        mask_m = sb("mask_m", [P, PAIR, LABELS, P])
        count = sb("count", [P, PAIR, LABELS])
        count_eps = sb("count_eps", [P, PAIR, LABELS])
        mean_w = sb("mean_w", [P, PAIR, LABELS])
        hT_full = sb("hT_full", [P, C, TOK])
        hT = pair("hT", [P, C, TOK])
        Y = pair("Y", [P, PAIR, LABELS * D])
        acc = sb("acc", [P, PAIR, D])
        acc2 = sb("acc2", [P, PAIR, D])
        oT = pair("oT", [P, C, TOK])
        r_gate = sb("r_gate", [P, C, TOK])
        z_gate = sb("z_gate", [P, C, TOK])
        hn = sb("hn", [P, C, TOK])
        pre = sb("pre", [P, C, TOK])
        n_gate = sb("n_gate", [P, C, TOK])
        diff, newT = hn, pre
        stats3 = sb("stats3", [P, PAIR, 6])
        mv3 = sb("mv3", [P, PAIR, 2])
        var3 = sb("var3", [P, PAIR])
        rstd3 = sb("rstd3", [P, PAIR])
        offset3 = sb("offset3", [P, PAIR])
        result = sb("result", [P, PAIR, D])

        bank = [ctx.enter_context(nc.psum_tensor(f"gbank{i}", [P, 512], F32)) for i in range(8)]
        load = sems("graw_landed0 graw_landed1 ghi_done glo_done gconst_landed setup_done fused_psum")
        ev = sems("gx_landed bo_done label_adj_landed label_adjT_landed maskT_done mask_m_done count_done count_eps_done mean_w_done "
                  "hT_psum hT_full hT_hi hT_lo "
                  "Y_psum Y_hi Y_lo sums half_mean mean "
                  "oT_psum oT_hi oT_lo r_psum r_tanh r_done z_psum z_tanh z_done nh_psum hn_done ni_psum pre_done "
                  "n_done diff_done zdiff_done newT_done new_psum new_rows stats3 mv3 var3 rstd3 offset3 z3 g3 result_done stored")
        block = ctx.enter_context(nc.Block())

        def halves(ap):
            return ap.rearrange("p (c t) -> p c t", c=2)

        @block.sync
        def _(sp):
            sp.dma_start(cols[:, :], cols_dram).then_inc(load["gconst_landed"], 16)
            sp.dma_start(rows[:, :, :], rows_dram.partition_broadcast(P)).then_inc(load["gconst_landed"], 16)
            for n in range(2, 5):
                sp.wait_ge(load["glo_done"], n - 1)
                if n == 3:
                    sp.wait_ge(load["fused_psum"], 2)
                width = min(CH, w_dram.shape[1] - n * CH)
                sp.dma_start(raw[:, n % 2, 0:width], w_dram[:, n * CH:n * CH + width]).then_inc(load[f"graw_landed{n % 2}"], 16)

            def load_adj(a):
                def piece(g):
                    wait(sp, a["mask_done"], g.before)
                    sp.dma_start(a.adj[:, :, :], adj_g[g.group]).then_inc(a["adj_landed"], 16)
                return piece

            def load_x2(g):
                wait(sp, A[0]["xr_done"], g.before)
                sp.dma_start(x_in[:, :, :], x2_g[g.group]).then_inc(ev["gx_landed"], 16)

            def load_labels(g):
                wait(sp, ev["maskT_done"], g.before)
                sp.dma_start(adjT_in[:, :, :], adjT_g[g.group]).then_inc(ev["label_adjT_landed"], 16)
                wait(sp, ev["mask_m_done"], g.before)
                sp.dma_start(adj_in[:, :, :], adj_g[g.group]).then_inc(ev["label_adj_landed"], 16)

            def store(g):
                sp.wait_ge(ev["result_done"], g.now)
                sp.dma_start(out_g[g.group], result[:, :, :]).then_inc(ev["stored"], 16)

            pipeline(sp, groups, GRAPH_ORDER["sp"], dict(
                load_x2=load_x2, load_adj_0=load_adj(A[0]), load_adj_1=load_adj(A[1]), load_adj_2=load_adj(A[2]),
                load_labels=load_labels, store=store))
            sp.wait_ge(ev["stored"], 16 * groups)

        @block.gpsimd
        def _(pool):
            pool.memset(power[:, :], -0.5).then_inc(load["setup_done"], 1)
            pool.memset(ident[:, :], 0.0).then_inc(load["setup_done"], 1)
            pool.wait_ge(load["setup_done"], 2)
            pool.affine_select(out=ident[:, :], in_=ident[:, :], compare_op=ALU.not_equal, fill=1.0, base=0,
                               pattern=[[-1, P]], channel_multiplier=1).then_inc(load["setup_done"], 1)
            pool.wait_ge(load["gconst_landed"], 32)
            for i in range(2):
                a = 4 + 4 * i
                last = pool.tensor_tensor(gate_sum[:, i, :], cols[:, a:a + C], cols[:, a + C:a + 2 * C], ALU.add)
            last.then_inc(load["setup_done"], 1)
            pool.wait_ge(load["setup_done"], 4)
            pool.tensor_scalar(gate_b[:, :, :], gate_sum[:, :, :], 0.5, None, ALU.mult).then_inc(load["setup_done"], 1)

            def row(i):
                return rows[:, i:i + 1, :].broadcast_to([P, PAIR, D])

            def mask(a):
                def piece(g):
                    pool.wait_ge(a["adj_landed"], bytes_landed(g.now))
                    wait(pool, a["peak"], g.before)
                    apart(pool)
                    pool.tensor_scalar(a.mask[:, :, :], a.adj[:, :, :], 0.0, MASKED, ALU.is_equal, ALU.mult).then_inc(a["mask_done"], 1)
                return piece

            def root(mv_done, mv, var_done, var, rstd_done, rstd):
                def piece(g):
                    pool.wait_ge(mv_done, g.now)
                    apart(pool)
                    pool.tensor_scalar(var[:, :], mv[:, :, 1], LN_EPS, None, ALU.add).then_inc(var_done, 1)
                    pool.wait_ge(var_done, g.now)
                    pool.tensor_tensor(rstd[:, :], var[:, :], power[:, :], ALU.pow).then_inc(rstd_done, 1)
                return piece

            def affine(dst, z, g_done, done, n):
                def piece(g):
                    pool.wait_ge(z, g.now)
                    pool.tensor_tensor(dst[:, :, :], dst[:, :, :], row(NORM_G[n]), ALU.mult).then_inc(g_done, 1)
                    pool.wait_ge(g_done, g.now)
                    pool.tensor_tensor(dst[:, :, :], dst[:, :, :], row(NORM_B[n]), ALU.add).then_inc(done, 1)
                return piece

            def x_plus_bo(g):
                pool.wait_ge(A[1]["x_done"], g.now)
                pool.tensor_tensor(x_bo[:, :, :], x[2][:, :, :], row(BO), ALU.add).then_inc(ev["bo_done"], 1)

            def label_masks(dst, src, landed, used, used_value, done):
                def piece(g):
                    pool.wait_ge(landed, bytes_landed(g.now))
                    wait(pool, used, used_value(g))
                    apart(pool)
                    for d in range(LABELS):
                        last = pool.tensor_scalar(dst[:, :, d, :], src[:, :, :], float(d + 1), None, ALU.is_equal)
                    last.then_inc(done, 1)
                return piece

            def sigmoid_of(t, tanh_done, done):
                def piece(g):
                    pool.wait_ge(tanh_done, g.now)
                    apart(pool)
                    pool.tensor_scalar(t[:, :, :], t[:, :, :], 0.5, 0.5, ALU.mult, ALU.add).then_inc(done, 1)
                return piece

            pieces = dict(
                x_plus_bo=x_plus_bo,
                maskT=label_masks(maskT, adjT_in, ev["label_adjT_landed"], ev["sums"], four_before, ev["maskT_done"]),
                mask_m=label_masks(mask_m, adj_in, ev["label_adj_landed"], ev["count_done"], lambda g: g.before, ev["mask_m_done"]),
                r_sigmoid=sigmoid_of(r_gate, ev["r_tanh"], ev["r_done"]), z_sigmoid=sigmoid_of(z_gate, ev["z_tanh"], ev["z_done"]),
                root_3=root(ev["mv3"], mv3, ev["var3"], var3, ev["rstd3"], rstd3),
                affine_3=affine(result, ev["z3"], ev["g3"], ev["result_done"], 3))
            for n, a in enumerate(A):
                pieces.update({f"mask_{n}": mask(a), f"root_{n}": root(a["mv"], a.mv, a["var"], a.var, a["rstd"], a.rstd),
                               f"affine_{n}": affine(x[n + 1], a["z"], a["g"], a["x_done"], n)})
            pipeline(pool, groups, GRAPH_ORDER["pool"], pieces)

        def flat(t):
            return t.rearrange("p a c n -> p (a c n)") if len(t.shape) == 4 else t.rearrange("p a n -> p (a n)")

        split_to = [(0, [flat(t[:, :, :]) for t in w1]), (2, [flat(t[:, :, :]) for t in wd]),
                    (3, [flat(t[:, :, :, :])[:, 0:CH] for t in wg]), (4, [flat(t[:, :, :, :])[:, CH:6 * C * D] for t in wg])]

        @block.scalar
        def _(act):
            for i, (n, w) in enumerate(split_to):
                if n >= 2:
                    act.wait_ge(load[f"graw_landed{n % 2}"], 16 * (n // 2))
                act.activation(w[0], raw[:, n % 2, 0:w[0].shape[1]], ACT.Copy).then_inc(load["ghi_done"], 1)
                if i == 0:
                    for k in range(2):
                        act.wait_ge(load["fused_psum"], k + 1)
                        act.activation(w2[0][:, k, :, :], halves(bank[k][:, :]), ACT.Copy).then_inc(load["ghi_done"], 1)
            act.wait_ge(load["gconst_landed"], 32)
            act.wait_ge(load["setup_done"], 5)

            def xT_hi(a):
                def piece(g):
                    act.wait_ge(a["xT_psum"], g.now)
                    if a.n == 2:
                        act.activation(a.xT_full[:, :, :], halves(bank[a.base][:, :]), ACT.Copy)
                    act.activation(a.xT[0][:, :, :], halves(bank[a.base][:, :]), ACT.Copy).then_inc(a["xT_hi"], 1)
                return piece

            def q_(a):
                def piece(g):
                    act.wait_ge(a["q_psum"], g.now)
                    if a.n < 2:
                        for i in range(2):
                            last = act.activation(a.q[:, i, :], bank[a.base][:, i * TOK:(i + 1) * TOK], ACT.Identity,
                                                  bias=cols[:, 2 * a.n + i:2 * a.n + i + 1])
                    else:
                        last = act.activation(a.q[:, :, :], halves(bank[a.base][:, :]), ACT.Copy)
                    last.then_inc(a["q_done"], 1)
                return piece

            def y_hi(a):
                def piece(g):
                    act.wait_ge(a["y_psum"], g.now)
                    act.activation(a.y[0][:, :, :], halves(bank[a.base + 1][:, :]), ACT.Copy).then_inc(a["y_hi"], 1)
                return piece

            def exps(a):
                def piece(g):
                    act.wait_ge(a["shift"], g.now)
                    for b in range(PAIR):
                        last = act.activation(a.prob[:, b, :], a.prob[:, b, :], ACT.Exp, bias=a.shift[:, b:b + 1],
                                              scale=score_scale[a.n], accum_out=a.total[:, b:b + 1])
                    last.then_inc(a["exp"], 1)
                return piece

            def probT_hi(a):
                def piece(g):
                    act.wait_ge(a["probT_psum"], g.now)
                    act.activation(a.probT[0][:, :, :], halves(bank[a.base + 1][:, 0:PAIR * P]), ACT.Copy).then_inc(a["probT_hi"], 1)
                return piece

            def hT_hi(g):
                act.wait_ge(ev["hT_psum"], g.now)
                wait(act, ev["diff_done"], g.before)
                act.activation(hT_full[:, :, :], halves(bank[6][:, :]), ACT.Copy)
                act.activation(hT[0][:, :, :], halves(bank[6][:, :]), ACT.Copy).then_inc(ev["hT_hi"], 1)

            def new_rows(g):
                act.wait_ge(ev["new_psum"], g.now)
                wait(act, ev["stored"], bytes_landed(g.before))
                act.activation(result[:, :, :], halves(bank[7][:, :]), ACT.Copy).then_inc(ev["new_rows"], 1)

            def Y_hi(i):
                def piece(g):
                    b, half = i // 2, i % 2
                    act.wait_ge(ev["Y_psum"], g.four[i])
                    act.activation(Y[0][:, b, half * 512:(half + 1) * 512], bank[6 + i % 2][:, :], ACT.Copy).then_inc(ev["Y_hi"], 1)
                return piece

            def oT_hi(g):
                act.wait_ge(ev["oT_psum"], g.now)
                act.activation(oT[0][:, :, :], halves(bank[6][:, :]), ACT.Relu).then_inc(ev["oT_hi"], 1)

            def apply(dst, src, rstd, offset, offset_done, z_done, used=None):
                def piece(g):
                    act.wait_ge(offset_done, g.now)
                    if used is not None:
                        wait(act, used, g.before)
                    for b in range(PAIR):
                        last = act.activation(dst[:, b, :], src[:, b, :], ACT.Identity, bias=offset[:, b:b + 1], scale=rstd[:, b:b + 1])
                    last.then_inc(z_done, 1)
                return piece

            def tanh(ready, dst, src, scale, bias, done):
                def piece(g):
                    act.wait_ge(ready, g.now)
                    for m in range(C):
                        last = act.activation(dst[:, m, :], src[:, m, :], ACT.Tanh, bias=bias[:, m:m + 1], scale=scale)
                    last.then_inc(done, 1)
                return piece

            pieces = dict(
                apply_3=apply(result, result, rstd3, offset3, ev["offset3"], ev["z3"]), new_rows=new_rows,
                hT_hi=hT_hi, Y_hi0=Y_hi(0), Y_hi1=Y_hi(1), Y_hi2=Y_hi(2), Y_hi3=Y_hi(3), oT_hi=oT_hi,
                r_tanh=tanh(ev["r_psum"], r_gate, halves(bank[7][:, :]), 0.5, gate_b[:, 0, :], ev["r_tanh"]),
                z_tanh=tanh(ev["z_psum"], z_gate, halves(bank[7][:, :]), 0.5, gate_b[:, 1, :], ev["z_tanh"]),
                n_tanh=tanh(ev["pre_done"], n_gate, pre, 1.0, cols[:, 12:14], ev["n_done"]))
            for n, a in enumerate(A):
                pieces.update({f"xT_hi_{n}": xT_hi(a), f"q_{n}": q_(a), f"y_hi_{n}": y_hi(a), f"exps_{n}": exps(a),
                               f"probT_hi_{n}": probT_hi(a),
                               f"apply_{n}": apply(x[n + 1], a.xr, a.rstd, a.offset, a["offset"], a["z"],
                                                    A[n + 1]["xr_done"] if n < 2 else None)})
            pipeline(act, groups, GRAPH_ORDER["act"], pieces)

        @block.vector
        def _(dve):
            for i, (n, w) in enumerate(split_to):
                dve.wait_ge(load["ghi_done"], i + 1 if i == 0 else i + 3)
                dve.tensor_tensor(w[1], raw[:, n % 2, 0:w[0].shape[1]], as_f32(w[0]), ALU.subtract).then_inc(load["glo_done"], 1)
                if i == 0:
                    for k in range(2):
                        dve.wait_ge(load["ghi_done"], k + 2)
                        last = dve.tensor_tensor(w2[1][:, k, :, :], halves(bank[k][:, :]), as_f32(w2[0][:, k, :, :]), ALU.subtract)
                    last.then_inc(load["glo_done"], 1)
            dve.wait_ge(load["gconst_landed"], 32)

            def norm_stats(src, stats, stats_done, mv, mv_done, g):
                for b in range(PAIR):
                    last = dve.bn_stats(stats[:, b, :], src[:, b, :])
                last.then_inc(stats_done, 1)
                dve.wait_ge(stats_done, g.now)
                apart(dve)
                for b in range(PAIR):
                    last = dve.bn_aggr(mv[:, b, :], stats[:, b, :])
                last.then_inc(mv_done, 1)

            def offset(mv, rstd, rstd_done, dst, done):
                def piece(g):
                    dve.wait_ge(rstd_done, g.now)
                    dve.scalar_tensor_tensor(out=dst[:, :], in0=mv[:, :, 0], scalar=-1.0, in1=rstd[:, :],
                                             op0=ALU.mult, op1=ALU.mult).then_inc(done, 1)
                return piece

            def xT_lo(a):
                def piece(g):
                    dve.wait_ge(a["xT_hi"], g.now)
                    dve.tensor_tensor(a.xT[1][:, :, :], halves(bank[a.base][:, :]), as_f32(a.xT[0][:, :, :]),
                                      ALU.subtract).then_inc(a["xT_lo"], 1)
                return piece

            def y_lo(a):
                def piece(g):
                    dve.wait_ge(a["y_hi"], g.now)
                    dve.tensor_tensor(a.y[1][:, :, :], halves(bank[a.base + 1][:, :]), as_f32(a.y[0][:, :, :]),
                                      ALU.subtract).then_inc(a["y_lo"], 1)
                return piece

            def peaks(a):
                def piece(g):
                    dve.wait_ge(a["scores"], g.now)
                    dve.wait_ge(a["mask_done"], g.now)
                    apart(dve)
                    for b in range(PAIR):
                        last = dve.tensor_tensor_reduce(a.prob[:, b, :], bank[a.base][:, b * P:(b + 1) * P], a.mask[:, b, :],
                                                        1.0, LOWEST, ALU.add, ALU.max, a.peak[:, b:b + 1])
                    last.then_inc(a["peak"], 1)
                    dve.wait_ge(a["peak"], g.now)
                    dve.tensor_scalar(a.shift[:, :], a.peak[:, :], -score_scale[a.n], None, ALU.mult).then_inc(a["shift"], 1)
                return piece

            def shares(a):
                def piece(g):
                    dve.wait_ge(a["exp"], g.now)
                    dve.reciprocal(a.inv[:, :], a.total[:, :]).then_inc(a["inv"], 1)
                    if a.n < 2:
                        dve.wait_ge(a["inv"], g.now)
                        dve.scalar_tensor_tensor(out=a.share[:, :], in0=a.peak[:, :], scalar=MASKED / 2, in1=a.inv[:, :],
                                                 op0=ALU.is_gt, op1=ALU.mult).then_inc(a["share"], 1)
                return piece

            def probT_lo(a):
                def piece(g):
                    dve.wait_ge(a["probT_hi"], g.now)
                    dve.tensor_tensor(a.probT[1][:, :, :], halves(bank[a.base + 1][:, 0:PAIR * P]), as_f32(a.probT[0][:, :, :]),
                                      ALU.subtract).then_inc(a["probT_lo"], 1)
                return piece

            def residual(a):
                def piece(g):
                    dve.wait_ge(a["ctx_psum"], g.now)
                    dve.wait_ge(a["share"], g.now)
                    res = x_bo if a.n == 2 else x[a.n]
                    if a.n == 2:
                        dve.wait_ge(ev["bo_done"], g.now)
                    for b in range(PAIR):
                        last = dve.scalar_tensor_tensor(out=a.xr[:, b, :], in0=bank[a.base][:, b * D:(b + 1) * D],
                                                        scalar=a.share[:, b:b + 1], in1=res[:, b, :], op0=ALU.mult, op1=ALU.add)
                    last.then_inc(a["xr_done"], 1)
                    dve.wait_ge(a["xr_done"], g.now)
                    norm_stats(a.xr, a.stats, a["stats"], a.mv, a["mv"], g)
                return piece

            def Y_lo(i):
                def piece(g):
                    b, half = i // 2, i % 2
                    dve.wait_ge(ev["Y_hi"], g.four[i])
                    dve.tensor_tensor(Y[1][:, b, half * 512:(half + 1) * 512], bank[6 + i % 2][:, :],
                                      as_f32(Y[0][:, b, half * 512:(half + 1) * 512]), ALU.subtract).then_inc(ev["Y_lo"], 1)
                return piece

            def counts(g):
                dve.tensor_reduce(count[:, :, :], mask_m[:, :, :, :], AX.X, ALU.add).then_inc(ev["count_done"], 1)
                dve.wait_ge(ev["count_done"], g.now)
                dve.tensor_scalar(count_eps[:, :, :], count[:, :, :], COUNT_EPS, None, ALU.add).then_inc(ev["count_eps_done"], 1)
                dve.wait_ge(ev["count_eps_done"], g.now)
                dve.reciprocal(mean_w[:, :, :], count_eps[:, :, :]).then_inc(ev["mean_w_done"], 1)

            def mean(i):
                def piece(g):
                    b, half = i // 2, i % 2
                    d = 2 * half
                    dve.wait_ge(ev["sums"], g.four[i])
                    if half == 1:
                        dve.wait_ge(ev["mean"], g.four[i - 1])
                    start = rows[:, BD, :] if half == 0 else acc[:, b, :]
                    dve.scalar_tensor_tensor(out=acc2[:, b, :], in0=bank[6 + i % 2][:, 0:D], scalar=mean_w[:, b, d:d + 1],
                                             in1=start, op0=ALU.mult, op1=ALU.add).then_inc(ev["half_mean"], 1)
                    dve.wait_ge(ev["half_mean"], g.four[i])
                    dve.scalar_tensor_tensor(out=acc[:, b, :], in0=bank[6 + i % 2][:, D:2 * D], scalar=mean_w[:, b, d + 1:d + 2],
                                             in1=acc2[:, b, :], op0=ALU.mult, op1=ALU.add).then_inc(ev["mean"], 1)
                return piece

            def hT_lo(g):
                dve.wait_ge(ev["hT_hi"], g.now)
                dve.tensor_tensor(hT[1][:, :, :], halves(bank[6][:, :]), as_f32(hT[0][:, :, :]), ALU.subtract).then_inc(ev["hT_lo"], 1)

            def oT_lo(g):
                dve.wait_ge(ev["oT_hi"], g.now)
                dve.scalar_tensor_tensor(out=oT[1][:, :, :], in0=halves(bank[6][:, :]), scalar=0.0, in1=as_f32(oT[0][:, :, :]),
                                         op0=ALU.max, op1=ALU.subtract).then_inc(ev["oT_lo"], 1)

            def gated_nh(g):
                dve.wait_ge(ev["nh_psum"], g.now)
                dve.wait_ge(ev["r_done"], g.now)
                for m in range(C):
                    last = dve.scalar_tensor_tensor(out=hn[:, m, :], in0=bank[6][:, m * TOK:(m + 1) * TOK], scalar=cols[:, 14 + m:15 + m],
                                                    in1=r_gate[:, m, :], op0=ALU.add, op1=ALU.mult)
                last.then_inc(ev["hn_done"], 1)

            def n_before_tanh(g):
                dve.wait_ge(ev["ni_psum"], g.now)
                dve.tensor_tensor(pre[:, :, :], halves(bank[6][:, :]), hn[:, :, :], ALU.add).then_inc(ev["pre_done"], 1)

            def blend(g):
                dve.wait_ge(ev["n_done"], g.now)
                dve.tensor_tensor(diff[:, :, :], hT_full[:, :, :], n_gate[:, :, :], ALU.subtract).then_inc(ev["diff_done"], 1)
                dve.wait_ge(ev["diff_done"], g.now)
                dve.wait_ge(ev["z_done"], g.now)
                dve.tensor_tensor(diff[:, :, :], diff[:, :, :], z_gate[:, :, :], ALU.mult).then_inc(ev["zdiff_done"], 1)
                dve.wait_ge(ev["zdiff_done"], g.now)
                dve.tensor_tensor(newT[:, :, :], diff[:, :, :], n_gate[:, :, :], ALU.add).then_inc(ev["newT_done"], 1)

            def stats_3(g):
                dve.wait_ge(ev["new_rows"], g.now)
                norm_stats(result, stats3, ev["stats3"], mv3, ev["mv3"], g)

            pieces = dict(
                hT_lo=hT_lo, Y_lo0=Y_lo(0), Y_lo1=Y_lo(1), Y_lo2=Y_lo(2), Y_lo3=Y_lo(3), counts=counts, mean0=mean(0), mean1=mean(1),
                mean2=mean(2), mean3=mean(3), oT_lo=oT_lo, gated_nh=gated_nh, n_before_tanh=n_before_tanh, blend=blend, stats_3=stats_3,
                offset_3=offset(mv3, rstd3, ev["rstd3"], offset3, ev["offset3"]))
            for n, a in enumerate(A):
                pieces.update({f"xT_lo_{n}": xT_lo(a), f"y_lo_{n}": y_lo(a), f"peaks_{n}": peaks(a), f"shares_{n}": shares(a),
                               f"probT_lo_{n}": probT_lo(a), f"residual_{n}": residual(a),
                               f"offset_{n}": offset(a.mv, a.rstd, a["rstd"], a.offset, a["offset"])})
            pipeline(dve, groups, GRAPH_ORDER["dve"], pieces)

        @block.tensor
        def _(pe):
            pe.wait_ge(load["setup_done"], 3)
            two = raw[:, 1, :].rearrange("p (w c n) -> p w c n", w=4, c=C)
            for k in range(2):
                for m in range(C):
                    for c in range(C):
                        last = pe.matmul(bank[k][:, m * D:(m + 1) * D], two[:, 2 * k, c, m * P:(m + 1) * P], two[:, 2 * k + 1, c, :],
                                         start=c == 0, stop=c == C - 1, skip_group_check=True)
                last.then_inc(load["fused_psum"], 1)
            pe.wait_ge(load["glo_done"], 5)

            def transposes(out, src):
                for c in range(C):
                    for b in range(PAIR):
                        last = pe.transpose(out[:, c * TOK + b * P:c * TOK + (b + 1) * P], src[:, b, c * P:(c + 1) * P], ident[:, :])
                return last

            def product(out, stationary, moving):
                for i, (s, m) in enumerate(zip(stationary, moving)):
                    last = split_product(pe, out, s, m, i == 0, i == len(stationary) - 1)
                return last

            def turned(a):
                def piece(g):
                    if a.n == 0:
                        pe.wait_ge(ev["gx_landed"], bytes_landed(g.now))
                    else:
                        pe.wait_ge(A[a.n - 1]["x_done"], g.now)
                    transposes(bank[a.base], x[a.n]).then_inc(a["xT_psum"], 1)
                return piece

            def q_(a):
                def piece(g):
                    pe.wait_ge(a["xT_lo"], g.now)
                    for i in range(2):
                        if a.n < 2:
                            w = [[t[:, a.n, i * 256 + c * P:i * 256 + (c + 1) * P] for t in w1] for c in range(C)]
                        else:
                            w = [[t[:, 0, c, i * P:(i + 1) * P] for t in w2] for c in range(C)]
                        last = product(bank[a.base][:, i * TOK:(i + 1) * TOK], w, [[t[:, c, :] for t in a.xT] for c in range(C)])
                    last.then_inc(a["q_psum"], 1)
                return piece

            def y_(a):
                def piece(g):
                    if a.n < 2:
                        w = [[t[:, a.n, 512 + c * D:512 + (c + 1) * D] for t in w1] for c in range(C)]
                    else:
                        w = [[t[:, 1, c, :] for t in w2] for c in range(C)]
                    for b in range(PAIR):
                        last = product(bank[a.base + 1][:, b * D:(b + 1) * D],
                                       [[t[:, c, b * P:(b + 1) * P] for t in a.xT] for c in range(C)], w)
                    last.then_inc(a["y_psum"], 1)
                return piece

            def scores(a):
                def piece(g):
                    pe.wait_ge(a["q_done"], g.now)
                    for b in range(PAIR):
                        tok = slice(b * P, (b + 1) * P)
                        if a.n < 2:
                            last = pe.matmul(bank[a.base][:, tok], a.q[:, 0, tok], a.q[:, 1, tok], start=True, stop=True, skip_group_check=True)
                        else:
                            for c in range(C):
                                last = pe.matmul(bank[a.base][:, tok], a.q[:, c, tok], a.xT_full[:, c, tok], start=c == 0, stop=c == C - 1, skip_group_check=True)
                    last.then_inc(a["scores"], 1)
                return piece

            def probs_turned(a):
                def piece(g):
                    pe.wait_ge(a["exp"], g.now)
                    pe.wait_ge(a["y_lo"], g.now)
                    for b in range(PAIR):
                        last = pe.transpose(bank[a.base + 1][:, b * P:(b + 1) * P], a.prob[:, b, :], ident[:, :])
                    last.then_inc(a["probT_psum"], 1)
                return piece

            def attend(a):
                def piece(g):
                    pe.wait_ge(a["probT_lo"], g.now)
                    for b in range(PAIR):
                        last = product(bank[a.base][:, b * D:(b + 1) * D], [[t[:, b, :] for t in a.probT]], [[t[:, b, :] for t in a.y]])
                    last.then_inc(a["ctx_psum"], 1)
                return piece

            def hid_turned(g):
                pe.wait_ge(A[2]["x_done"], g.now)
                wait(pe, ev["pre_done"], g.before)
                transposes(bank[6], x[3]).then_inc(ev["hT_psum"], 1)

            def labels(i):
                def piece(g):
                    b, half = i // 2, i % 2
                    if i < 2:
                        pe.wait_ge(ev["hT_lo"], g.now)
                    if i == 1:
                        wait(pe, ev["new_rows"], g.before)
                    if i >= 2:
                        pe.wait_ge(ev["Y_lo"], g.four[i - 2])
                    product(bank[6 + i % 2][:, :], [[t[:, c, b * P:(b + 1) * P] for t in hT] for c in range(C)],
                            [[t[:, c, half * 512:(half + 1) * 512] for t in wd] for c in range(C)]).then_inc(ev["Y_psum"], 1)
                return piece

            def sums(i):
                def piece(g):
                    b, half = i // 2, i % 2
                    if i < 2:
                        pe.wait_ge(ev["Y_lo"], g.four[i + 2])
                    else:
                        pe.wait_ge(ev["mean"], g.four[i - 2])
                    for k in range(2):
                        d = 2 * half + k
                        for part in (1, 0):
                            last = pe.matmul(bank[6 + i % 2][:, k * D:(k + 1) * D], maskT[:, b, d, :], Y[part][:, b, d * D:(d + 1) * D],
                                             start=part == 1, stop=part == 0, skip_group_check=True)
                    last.then_inc(ev["sums"], 1)
                return piece

            def out_turned(g):
                pe.wait_ge(ev["mean"], g.four[3])
                transposes(bank[6], acc).then_inc(ev["oT_psum"], 1)

            def gate(out, i_w, h_w, done, waits):
                def piece(g):
                    for sem in waits:
                        pe.wait_ge(sem, g.now)
                    for m in range(C):
                        s, mv = [], []
                        for w, act_ in ((i_w, oT), (h_w, hT)):
                            if w is not None:
                                s += [[t[:, w, c, m * P:(m + 1) * P] for t in wg] for c in range(C)]
                                mv += [[t[:, c, :] for t in act_] for c in range(C)]
                        last = product(out[:, m * TOK:(m + 1) * TOK], s, mv)
                    last.then_inc(done, 1)
                return piece

            def new_turned(g):
                pe.wait_ge(ev["newT_done"], g.now)
                for b in range(PAIR):
                    for c in range(C):
                        last = pe.transpose(bank[7][:, b * D + c * P:b * D + (c + 1) * P], newT[:, c, b * P:(b + 1) * P], ident[:, :])
                last.then_inc(ev["new_psum"], 1)

            pieces = dict(
                hid_turned=hid_turned, labels0=labels(0), labels1=labels(1), labels2=labels(2), labels3=labels(3),
                sums0=sums(0), sums1=sums(1), sums2=sums(2), sums3=sums(3), out_turned=out_turned,
                r=gate(bank[7], 0, 1, ev["r_psum"], [ev["oT_lo"]]), nh=gate(bank[6], None, 5, ev["nh_psum"], []),
                z=gate(bank[7], 2, 3, ev["z_psum"], [ev["r_tanh"]]), ni=gate(bank[6], 4, None, ev["ni_psum"], [ev["hn_done"]]),
                new_turned=new_turned)
            for n, a in enumerate(A):
                pieces.update({f"turned_{n}": turned(a), f"q_{n}": q_(a), f"y_{n}": y_(a), f"scores_{n}": scores(a),
                               f"probs_turned_{n}": probs_turned(a), f"attend_{n}": attend(a)})
            pipeline(pe, groups, GRAPH_ORDER["pe"], pieces)


def build(nc, x, adj, adjT, w_a, cols_a, rows_a, w_b, cols_b, rows_b, out):
    x2 = nc.dram_tensor("x2_rows", x.shape, F32, kind="Internal").ap()
    with ExitStack() as ctx:
        raw = ctx.enter_context(nc.sbuf_tensor("raw", [P, 2, CH], F32))
        taken = encoder_phase(nc, x, adj, w_a, cols_a, rows_a, x2, raw, w_b)
        nc.all_engine_barrier()
        nc.clear_and_free_semaphores(taken)
        nc.all_engine_barrier()
        graph_phase(nc, x2, adj, adjT, w_b, cols_b, rows_b, out, raw)


def kernel(**inputs):
    import numpy as np
    import concourse.bacc as bacc
    from concourse.bass_utils import run_bass_kernel_spmd

    a = {k: np.asarray(v) for k, v in inputs.items()}

    def chunks(w):
        return w.reshape(-1, P, w.shape[1]).transpose(1, 0, 2).reshape(P, -1)

    def col(v):
        return v.reshape(-1, P).T

    L0, L1, L2, L3 = "L0_gnn_", "L1_gnn_", "L2_gnn_", "L3_gnn_"
    w_a = np.concatenate([chunks(a[L0 + n]) for n in ("wq", "wk", "wv", "wo", "w1", "w2")], axis=1)
    cols_a = np.concatenate([col(a[L0 + n]) for n in ("bq", "bk", "b1")], axis=1)
    rows_a = np.stack([a[L0 + n] for n in ("ln1_g", "ln1_b", "bv", "bo", "ln2_g", "ln2_b", "b2")])
    wd = a[L3 + "Wd"].reshape(D, LABELS, D).transpose(2, 1, 0).reshape(D, LABELS * D)
    w_b = np.concatenate(
        [chunks(a[L1 + n][l].T) for l in range(2) for n in ("Wq", "Wk", "Wc")]
        + [chunks(a[L2 + "Wq"].T), chunks(a[L2 + "Wk"].T), chunks(a[L2 + "Wv"].T), chunks(a[L2 + "Wo"]), chunks(wd)]
        + [chunks(a[L3 + n].T) for n in ("Wri", "Wrh", "Wzi", "Wzh", "Wni", "Wnh")], axis=1)
    cols_b = np.concatenate([col(a[L1 + n][l]) for l in range(2) for n in ("bq", "bk")]
                            + [col(a[L3 + n]) for n in ("bri", "brh", "bzi", "bzh", "bni", "bnh")], axis=1)
    rows_b = np.stack([a[L1 + "ln_g"][0], a[L1 + "ln_b"][0], a[L1 + "ln_g"][1], a[L1 + "ln_b"][1], a[L2 + "bo"],
                       a[L2 + "gamma"], a[L2 + "beta"], a[L3 + "bd"], a[L3 + "gamma"], a[L3 + "beta"]])
    laid = {"x": a["x"], "adj": a["adj"], "adjT": a["adj"].transpose(0, 2, 1), "w_a": w_a, "cols_a": cols_a,
            "rows_a": rows_a, "w_b": w_b, "cols_b": cols_b, "rows_b": rows_b}
    laid = {"in_" + k: np.ascontiguousarray(v) for k, v in laid.items()}

    nc = bacc.Bacc("TRN2", target_bir_lowering=False, num_devices=1)
    args = [nc.dram_tensor(k, v.shape, mybir.dt.from_np(v.dtype), kind="ExternalInput").ap() for k, v in laid.items()]
    out = nc.dram_tensor("out_rows", a["x"].shape, F32, kind="ExternalOutput").ap()
    build(nc, *args, out)
    r = run_bass_kernel_spmd(nc, [laid], core_ids=[0])
    return r.results[0]["out_rows"]
```
